# Optimizing a Trainium2 kernel written in Bass

```python
import numpy as np
import jax
import jax.numpy as jnp

def _softmax(x, axis=-1):
    return jax.nn.softmax(x, axis=axis)

def _gelu(x):
    return jax.nn.gelu(x, approximate=True)

def _silu(x):
    return jax.nn.silu(x)

def _sigmoid(x):
    return jax.nn.sigmoid(x)

def _layernorm(x, axis=-1, eps=1e-05):
    m = jnp.mean(x, axis=axis, keepdims=True)
    v = jnp.var(x, axis=axis, keepdims=True)
    return (x - m) / jnp.sqrt(v + eps)

def _scatter_add(tgt, idx, src, axis=0):
    return tgt.at[idx].add(src)

def _segment_sum(src, seg, n):
    return jax.ops.segment_sum(src, seg, n)
kernel_name = 'mk_gps_d1_gnn_r8_274874'

def setup_inputs(seed: int=0):
    np.random.seed(seed)
    _w = jnp.asarray

    def _rec_inputs():
        import jax
        import jax.numpy as jnp
        _gk = jax.random.key(seed)
        x = -0.0003713 + 1 * jax.random.normal(jax.random.fold_in(_gk, 1), (6250, 256), jnp.float32)
        _s = jax.random.randint(jax.random.fold_in(_gk, 2), (50000,), 0, 6250, jnp.int32)
        _d = jax.random.randint(jax.random.fold_in(_gk, 3), (50000,), 0, 6250, jnp.int32)
        _loop = jnp.arange(6250, dtype=jnp.int32)
        src = jnp.concatenate([_s, _d, _loop])
        dst = jnp.concatenate([_d, _s, _loop])
        _o = jnp.argsort(dst, stable=True)
        src = src[_o]
        dst = dst[_o]
        return (x, src, dst)
    x, src, dst = _rec_inputs()

    def _L0_gnn_setup():
        import jax, jax.numpy as jnp
        import numpy as np
        N, E, D_IN, D_OUT = (6250, 200000, 256, 256)
        key = jax.random.key(seed)
        k1, k2, k3, k4, k5, k6 = jax.random.split(key, 6)
        x = jax.random.normal(k1, (N, D_IN), dtype=jnp.float32)
        edge_index = jax.random.randint(k2, (2, E), 0, N, dtype=jnp.int64)
        s = 1.0 / np.sqrt(D_IN)
        W1 = jax.random.uniform(k3, (D_OUT, D_IN), minval=-s, maxval=s, dtype=jnp.float32)
        b1 = jax.random.uniform(k4, (D_OUT,), minval=-s, maxval=s, dtype=jnp.float32)
        W2 = jax.random.uniform(k5, (D_OUT, D_IN), minval=-s, maxval=s, dtype=jnp.float32)
        b2 = jax.random.uniform(k6, (D_OUT,), minval=-s, maxval=s, dtype=jnp.float32)
        return {'x': x, 'W1': W1, 'b1': b1, 'W2': W2, 'b2': b2, 'edge_index': edge_index}
    _L0_gnn_all = _L0_gnn_setup()
    _L0_gnn_in = {k: v for k, v in _L0_gnn_all.items() if k in ('W1', 'b1', 'W2', 'b2')}
    del _L0_gnn_all

    def _L0_mix_setup():
        import jax, jax.numpy as jnp
        import numpy as np
        NUM_HEADS = 8
        key = jax.random.key(seed)
        ks = jax.random.split(key, 5)
        B, N, C = (8, 2048, 256)
        x = jax.random.normal(ks[0], (B, N, C), dtype=jnp.float32)
        Wq = jax.random.normal(ks[1], (C, C), dtype=jnp.float32) * 0.02
        Wkv = jax.random.normal(ks[2], (2 * C, C), dtype=jnp.float32) * 0.02
        Wproj = jax.random.normal(ks[3], (C, C), dtype=jnp.float32) * 0.02
        bproj = jnp.zeros((C,), dtype=jnp.float32)
        return {'x': x, 'Wq': Wq, 'Wkv': Wkv, 'Wproj': Wproj, 'bproj': bproj}
    _L0_mix_all = _L0_mix_setup()
    _L0_mix_in = {k: v for k, v in _L0_mix_all.items() if k in ('Wq', 'Wkv', 'Wproj', 'bproj')}
    del _L0_mix_all

    def _L0_ffn_setup():
        import jax, jax.numpy as jnp
        import numpy as np
        B, K, D = (512, 16, 256)
        E = 32
        H = int(D * 0.25)
        key = jax.random.key(seed)
        ks = jax.random.split(key, 7)
        d_rs = D ** (-0.5)
        h_rs = H ** (-0.5)
        x = jax.random.normal(ks[0], (B, K, D), dtype=jnp.float32)
        router_w = jax.random.uniform(ks[1], (E, D), jnp.float32, -d_rs, d_rs)
        router_b = jax.random.uniform(ks[2], (E,), jnp.float32, -d_rs, d_rs)
        W1 = jax.random.uniform(ks[3], (E, D, H), jnp.float32, -h_rs, h_rs)
        b1 = jax.random.uniform(ks[4], (E, H), jnp.float32, -h_rs, h_rs)
        W2 = jax.random.uniform(ks[5], (E, H, D), jnp.float32, -d_rs, d_rs)
        b2 = jax.random.uniform(ks[6], (E, D), jnp.float32, -d_rs, d_rs)
        return {'x': x, 'router_w': router_w, 'router_b': router_b, 'W1': W1, 'b1': b1, 'W2': W2, 'b2': b2}
    _L0_ffn_all = _L0_ffn_setup()
    _L0_ffn_in = {k: v for k, v in _L0_ffn_all.items() if k in ('router_w', 'router_b', 'W1', 'b1', 'W2', 'b2')}
    del _L0_ffn_all
    return {'x': x, 'src': src, 'dst': dst, 'L0_gnn_W1': _L0_gnn_in['W1'], 'L0_gnn_b1': _L0_gnn_in['b1'], 'L0_gnn_W2': _L0_gnn_in['W2'], 'L0_gnn_b2': _L0_gnn_in['b2'], 'L0_mix_Wq': _L0_mix_in['Wq'], 'L0_mix_Wkv': _L0_mix_in['Wkv'], 'L0_mix_Wproj': _L0_mix_in['Wproj'], 'L0_mix_bproj': _L0_mix_in['bproj'], 'L0_ffn_router_w': _L0_ffn_in['router_w'], 'L0_ffn_router_b': _L0_ffn_in['router_b'], 'L0_ffn_W1': _L0_ffn_in['W1'], 'L0_ffn_b1': _L0_ffn_in['b1'], 'L0_ffn_W2': _L0_ffn_in['W2'], 'L0_ffn_b2': _L0_ffn_in['b2']}

def reference(x, src, dst, L0_gnn_W1, L0_gnn_b1, L0_gnn_W2, L0_gnn_b2, L0_mix_Wq, L0_mix_Wkv, L0_mix_Wproj, L0_mix_bproj, L0_ffn_router_w, L0_ffn_router_b, L0_ffn_W1, L0_ffn_b1, L0_ffn_W2, L0_ffn_b2):
    import jax
    import jax.numpy as jnp

    def _L0_gnn_ref(x, W1, b1, W2, b2, edge_index):
        import jax, jax.numpy as jnp
        import numpy as np
        N, E, D_IN, D_OUT = (6250, 200000, 256, 256)
        dst = edge_index[0]
        nbr = edge_index[1]
        n = x.shape[0]
        agg = jax.ops.segment_sum(x[nbr], dst, num_segments=n)
        cnt = jax.ops.segment_sum(jnp.ones((nbr.shape[0],), x.dtype), dst, num_segments=n)
        mean = agg / jnp.maximum(cnt, 1.0)[:, None]
        return x @ W1.T + b1 + mean @ W2.T + b2

    def _L0_mix_ref(x, Wq, Wkv, Wproj, bproj):
        import jax, jax.numpy as jnp
        import numpy as np
        NUM_HEADS = 8
        B, N, C = x.shape
        h = NUM_HEADS
        d = C // h
        q = jnp.einsum('bnc,oc->bno', x, Wq).reshape(B, N, h, d).transpose(0, 2, 1, 3)
        kv = jnp.einsum('bnc,oc->bno', x, Wkv).reshape(B, N, 2, h, d)
        k = kv[:, :, 0].transpose(0, 2, 1, 3)
        v = kv[:, :, 1].transpose(0, 2, 1, 3)
        q = jax.nn.elu(q) + 1.0
        k = jax.nn.elu(k) + 1.0
        k_sum = k.sum(axis=2)
        D_inv = 1.0 / jnp.maximum(jnp.einsum('bhnd,bhd->bhn', q, k_sum), 1e-06)
        context = jnp.einsum('bhnd,bhne->bhde', k, v)
        attn = jnp.einsum('bhnd,bhde->bhne', q, context) * D_inv[..., None]
        out = attn.transpose(0, 2, 1, 3).reshape(B, N, C)
        out = jnp.einsum('bnc,oc->bno', out, Wproj) + bproj
        return out

    def _L0_ffn_ref(x, router_w, router_b, W1, b1, W2, b2):
        import jax, jax.numpy as jnp
        import numpy as np
        B, K, D = (512, 16, 256)
        E = 32
        H = int(D * 0.25)
        xf = x.reshape(-1, D)
        logits = xf @ router_w.T + router_b
        idx = jnp.argmax(logits, axis=-1)
        w1t = jnp.take(W1, idx, axis=0)
        h = jnp.einsum('nd,ndh->nh', xf, w1t) + jnp.take(b1, idx, axis=0)
        h = jax.nn.relu(h)
        w2t = jnp.take(W2, idx, axis=0)
        out = jnp.einsum('nh,nhd->nd', h, w2t) + jnp.take(b2, idx, axis=0)
        out = jax.nn.relu(out)
        return out.reshape(x.shape)
    edge_index = jnp.stack([src, dst])
    xn = _layernorm(x, axis=-1)
    x = x + _L0_gnn_ref(xn, L0_gnn_W1, L0_gnn_b1, L0_gnn_W2, L0_gnn_b2, edge_index) + _L0_mix_ref(xn[None], L0_mix_Wq, L0_mix_Wkv, L0_mix_Wproj, L0_mix_bproj)[0]
    x = x + _L0_ffn_ref(_layernorm(x, axis=-1)[None], L0_ffn_router_w, L0_ffn_router_b, L0_ffn_W1, L0_ffn_b1, L0_ffn_W2, L0_ffn_b2)[0]
    return x

_drawn_inputs = setup_inputs


def setup_inputs(seed=0):
    import zlib

    import numpy as np

    out = dict(_drawn_inputs(seed))
    spreads = {'L0_mix_bproj': (0.0, 0.1)}
    factors = {'L0_mix_Wq': 8.0,
     'L0_mix_Wkv': 8.0,
     'L0_mix_Wproj': 8.0,
     'L0_ffn_b1': 6.701,
     'L0_ffn_b2': 2.692}
    for name, (base, spread) in spreads.items():
        noise = np.random.default_rng([zlib.crc32(name.encode()), seed]).standard_normal(out[name].shape)
        drawn = base * np.exp(spread * noise) if base else spread * noise
        out[name] = jnp.asarray(drawn.astype(out[name].dtype))
    for name, factor in factors.items():
        out[name] = (out[name] * factor).astype(out[name].dtype)
    return out
```

```python
from contextlib import ExitStack

import concourse.bass as bass
from concourse import mybir

ALU = mybir.AluOpType
ACT = mybir.ActivationFunctionType
F32 = mybir.dt.float32
I32 = mybir.dt.int32
U32 = mybir.dt.uint32

N, D = 6250, 256
NB, NS = 125, 50
E, EC = 106250, 832
HEADS, DH = 8, 32
NE, H = 32, 64
JH = NE * H // 128
G = NS // 2
PASS = 5
UN = 8
EPS = 1e-5
BIG = 1e30


def wait(eng, sem, value):
    if isinstance(value, int) and value <= 0:
        return
    eng.wait_ge(sem, value)


def run(eng, n, stages, peel=4):
    lag = max(l for l, _ in stages)
    half = (n - peel) // 2

    def static(step):
        for l, work in stages:
            if 0 <= step - l < n:
                work(step - l, (step - l) % 2)

    for step in range(peel):
        static(step)
    with eng.Fori(0, half) as i:
        for u in range(2):
            for l, work in stages:
                work(i * 2 + (peel + u - l), (peel + u - l) % 2)
    for step in range(peel + 2 * half, n + lag):
        static(step)


def gps_layer(nc, x, src, dst, wkv, wyz, wq, wproj, bias3, rw, rb, w1, b1, w2, b2, out):
    y_table = nc.dram_tensor("y_table", [N, D], F32).ap()
    with ExitStack() as ctx:
        def sb(name, shape, dt=F32):
            return ctx.enter_context(nc.sbuf_tensor(name, shape, dt))

        def sem(name):
            return ctx.enter_context(nc.semaphore(name))

        ps = ctx.enter_context(nc.psum_tensor("ps", [128, 8, 512], F32))

        arena = sb("arena", [128, 6000])

        def part(at, p, *shape):
            size = 1
            for k in shape:
                size *= k
            names = [f"a{k}" for k in range(len(shape))]
            flat = arena[0:p, at:at + size]
            if len(shape) == 1:
                return flat
            return flat.rearrange(f"p ({' '.join(names)}) -> p {' '.join(names)}", **{m: k for m, k in zip(names, shape)})

        x_sb = sb("x_sb", [NB, NS, D])
        agg_sb = sb("agg_sb", [NB, NS, D + 1])
        xnT = sb("xnT", [128, 2, N])
        wkv_sb = part(0, 128, 2, 2 * D)
        wyz_sb = part(1024, 128, 2, 2 * D)
        wq_sb = sb("wq_sb", [128, 2, D])
        wp_sb = sb("wp_sb", [128, 2, D])
        bias_sb = sb("bias_sb", [128, 3, D])
        bias = sb("bias", [128, D])
        biast = sb("biast", [128, D])
        ident = sb("ident", [128, 128])
        st = sb("st", [NB, 2, 6])
        mv = sb("mv", [NB, 2, 2])
        rs = sb("rs", [NB, 2])
        ve = sb("ve", [NB, 2])
        mhalf = sb("mhalf", [128, 1])
        xn = part(2048, NB, 2, D)
        xt = part(2560, 128, 2, 2, NB)
        km = part(3060, NB, 2, D)
        kx = part(3572, NB, 2, D)
        kf = part(4084, NB, 2, D)
        vv = part(4596, NB, 2, D + 2)
        cx = sb("cx", [128, 2, 129])
        cbd = sb("cbd", [128, 2, 128])
        cbdT = sb("cbdT", [128, 2, 128])
        hmask = sb("hmask", [128, 128])
        hm0 = sb("hm0", [128, 128])
        ksb = sb("ksb", [128, 2, 128])
        msb = sb("msb", [128, 2, D])
        src_i = sb("src_i", [128, EC], I32)
        dst_i = sb("dst_i", [128, EC], I32)
        srcf = src_i[:, :].bitcast(F32)
        nodes = sb("nodes", [128, PASS, NB])
        ixb = sb("ixb", [128, 2, UN // 2], U32)
        grow = part(0, 128, UN, D + 1)
        oneh = part(2056, 128, 2, PASS * NB)

        s_in, s_w, s_id, s_c = sem("s_in"), sem("s_w"), sem("s_id"), sem("s_c")
        v_bias, v_st, v_ag, v_rs, v_xn = sem("v_bias"), sem("v_st"), sem("v_ag"), sem("v_rs"), sem("v_xn")
        p_b, pe_tr, a_xt, a_xt2, pe_kv, pe_yz = sem("p_b"), sem("pe_tr"), sem("a_xt"), sem("a_xt2"), sem("pe_kv"), sem("pe_yz")
        v_km, a_kx, v_kf, a_v, a_y, v_base, pe_cx = (sem(n) for n in ("v_km", "a_kx", "v_kf", "a_v", "a_y", "v_base", "pe_cx"))
        y_out, v_cx, v_cm, pe_ct, v_ct, pe_m, v_m = (sem(n) for n in ("y_out", "v_cx", "v_cm", "pe_ct", "v_ct", "pe_m", "v_m"))
        pe_q, v_qm, a_qx, v_qf, pe_dn, v_dn, v_rc, v_qs, pe_at, v_at = (sem(n) for n in (
            "pe_q", "v_qm", "a_qx", "v_qf", "pe_dn", "v_dn", "v_rc", "v_qs", "pe_at", "v_at"))
        s_e, v_e, p_ix, p_z, v_sub, v_oh, pe_e, pe_pass, v_agg = (sem(n) for n in (
            "s_e", "v_e", "p_ix", "p_z", "v_sub", "v_oh", "pe_e", "pe_pass", "v_agg"))
        g_in = [sem(f"g_in{k}") for k in range(UN)]
        s_f, p_ve = sem("s_f"), sem("p_ve")
        f_c, f_rc, f_x1, f_st, f_ag, f_rs, f_xf = (sem(n) for n in ("f_c", "f_rc", "f_x1", "f_st", "f_ag", "f_rs", "f_xf"))
        f_tr, f_xt, f_lg, f_lb, f_mx, f_ix, f_if, f_oh, f_ot, f_os, f_h, f_hs, f_o, f_r, f_y = (sem(n) for n in (
            "f_tr", "f_xt", "f_lg", "f_lb", "f_mx", "f_ix", "f_if", "f_oh", "f_ot", "f_os", "f_h", "f_hs", "f_o", "f_r", "f_y"))
        f_out = sem("f_out")
        alone_v, alone_gp = sem("alone_v"), sem("alone_gp")

        xnT_flat = xnT[:, :, :].rearrange("p a b -> p (a b)")
        w1_sb = xnT_flat[:, 0:2 * NE * H].rearrange("p (c j) -> p c j", c=2)
        w2_sb = xnT_flat[:, 4096:4096 + JH * D].rearrange("p (j d) -> p j d", j=JH)
        hs = xnT_flat[:, 8192:8192 + JH * 250].rearrange("p (j n) -> p j n", j=JH)
        rw_sb = sb("rw_sb", [128, 2, NE])
        rb_sb = sb("rb_sb", [128, NE])
        b1_sb = sb("b1_sb", [128, JH])
        b2_sb = sb("b2_sb", [NE, D])
        off0 = part(3306, NE, NE * H)
        iota_e = sb("iota_e", [128, NE])
        rc = sb("rc", [NB, NS])
        rc0 = sb("rc0", [NB, NS])
        xfT = sb("xfT", [128, 2, 2, NB])
        lg = sb("lg", [NB, 2, NE])
        mx = sb("mx", [NB, 2, 8])
        mi = sb("mi", [NB, 2, 8], U32)
        mf = sb("mf", [NB, 2, 1])
        oe = sb("oe", [NB, 2, NE])
        oeT = sb("oeT", [NE, 2, NB])
        fst = sb("fst", [NB, 2, 6])
        fmv = sb("fmv", [NB, 2, 2])
        frs = sb("frs", [NB, 2])
        fxf = sb("fxf", [NB, 2, D])

        qm = [part(0 + 500 * k, 128, 500) for k in range(2)]
        qx = [part(1000 + 500 * k, 128, 500) for k in range(2)]
        qf = [part(2000 + 500 * k, 128, 500) for k in range(2)]
        dn = [part(3000 + 500 * k, 128, 500) for k in range(2)]
        qs = [part(4000 + 500 * k, 128, 500) for k in range(2)]
        qm2 = [part(5000 + 500 * k, 128, 500) for k in range(2)]

        x_v = x.rearrange("(b s) d -> b s d", s=NS)
        y_v = y_table.rearrange("(b s) d -> b s d", s=NS)
        o_v = out.rearrange("(b s) d -> b s d", s=NS)
        HALVES = ((0, 112), (112, NB))

        block = ctx.enter_context(nc.Block())

        @block.sync
        def _(sp):
            for a, b in HALVES:
                sp.dma_start(x_sb[a:b], x_v[a:b]).then_inc(s_in, 16)
            for k, (t, w) in enumerate(((wkv_sb, wkv), (wyz_sb, wyz), (wq_sb, wq), (wp_sb, wproj))):
                sp.dma_start(t[:], w.rearrange("(c p) o -> p c o", p=128)).then_inc(s_w, 16)
            sp.dma_start(bias_sb[:], bias3.rearrange("a d -> () a d").to_broadcast([128, 3, D])).then_inc(s_w, 16)
            full = E // EC
            sp.wait_ge(v_e, 2)
            for t, w in ((src_i, src), (dst_i, dst)):
                sp.dma_start(t[0:full], w[0:full * EC].rearrange("(p c) -> p c", c=EC)).then_inc(s_e, 16)
                sp.dma_start(t[full:full + 1, 0:E - full * EC],
                             w[full * EC:E].rearrange("(p c) -> p c", p=1)).then_inc(s_e, 16)
            for k in range(5):
                sp.wait_ge(a_y, 10 * (k + 1))
                for a, b in HALVES:
                    sp.dma_start(y_v[a:b, 10 * k:10 * k + 10], agg_sb[a:b, 10 * k:10 * k + 10, 0:D]).then_inc(y_out, 16)
            sp.wait_ge(pe_q, G)
            for c in range(2):
                sp.dma_start(w1_sb[:, c].rearrange("p (e h) -> p e h", e=NE),
                             w1[:, c * 128:(c + 1) * 128].rearrange("e p h -> p e h")).then_inc(s_f, 16)
            sp.dma_start(w2_sb, w2.rearrange("(j p) d -> p j d", p=128)).then_inc(s_f, 16)
            sp.dma_start(rw_sb[:], rw.rearrange("(c p) o -> p c o", p=128)).then_inc(s_f, 16)
            sp.dma_start(rb_sb[:], rb.rearrange("n -> () n").to_broadcast([128, NE])).then_inc(s_f, 16)
            sp.dma_start(b1_sb[:], b1).then_inc(s_f, 16)
            sp.dma_start(b2_sb[:], b2).then_inc(s_f, 16)
            for k in range(5):
                sp.wait_ge(f_y, 10 * (k + 1))
                for a, b in HALVES:
                    sp.dma_start(o_v[a:b, 10 * k:10 * k + 10], x_sb[a:b, 10 * k:10 * k + 10]).then_inc(f_out, 16)
            sp.wait_ge(f_out, 160)

        @block.gpsimd
        def _(gp):
            gp.memset(ident[:], 0.0).then_inc(s_id, 1)
            gp.memset(hm0[:], 1.0).then_inc(s_id, 1)
            gp.wait_ge(s_id, 2)
            gp.affine_select(out=ident[:], in_=ident[:], compare_op=ALU.not_equal, fill=1.0, base=0,
                             pattern=[[-1, 128]], channel_multiplier=1).then_inc(s_id, 1)
            gp.affine_select(out=hm0[:].rearrange("p (a b) -> p a b", b=DH), in_=hm0[:].rearrange("p (a b) -> p a b", b=DH),
                             compare_op=ALU.is_ge, fill=0.0, base=0,
                             pattern=[[-DH, 128 // DH], [0, DH]], channel_multiplier=1).then_inc(s_id, 1)
            gp.wait_ge(s_id, 4)
            gp.affine_select(out=hmask[:].rearrange("p (a b) -> p a b", b=DH), in_=hm0[:].rearrange("p (a b) -> p a b", b=DH),
                             compare_op=ALU.is_ge, fill=0.0, base=DH - 1,
                             pattern=[[DH, 128 // DH], [0, DH]], channel_multiplier=-1).then_inc(s_id, 1)
            gp.iota(nodes[:], [[1, PASS], [NS, NB]], base=0, channel_multiplier=0,
                    allow_small_or_imprecise_dtypes=True).then_inc(s_id, 1)
            gp.iota(iota_e[:], [[1, NE]], base=0, channel_multiplier=0,
                    allow_small_or_imprecise_dtypes=True).then_inc(s_id, 1)
            gp.memset(vv[:], 1.0).then_inc(s_id, 1)
            gp.memset(mhalf[:], -0.5).then_inc(s_id, 1)
            gp.wait_ge(s_id, 9)

            def add_bias(s, par):
                gp.wait_ge(v_ag, s + 1)
                gp.sem_inc(alone_gp, 1)
                gp.tensor_scalar(ve[:, par:par + 1], mv[:, par, 1:2], EPS, None, ALU.add).then_inc(p_ve, 1)
                gp.wait_ge(p_ve, s + 1)
                gp.tensor_tensor(rs[:, par:par + 1], ve[:, par:par + 1], mhalf[0:NB], ALU.pow).then_inc(v_rs, 1)
                gp.wait_ge(v_xn, s + 1)
                gp.tensor_tensor(x_sb[:, s, :], x_sb[:, s, :], bias[0:NB], ALU.add).then_inc(p_b, 1)

            gp.wait_ge(v_bias, 2)
            run(gp, NS, [(0, add_bias)])
            gp.wait_ge(s_e, 64)
            gp.wait_ge(y_out, 160)
            gp.wait_ge(v_at, G)
            gp.memset(grow[:], 1.0).then_inc(s_c, 1)
            gp.memset(off0[:], 0.0).then_inc(s_c, 1)
            gp.wait_ge(s_c, 2)
            gp.affine_select(out=off0[:].rearrange("p (a b) -> p a b", b=H), in_=off0[:].rearrange("p (a b) -> p a b", b=H),
                             compare_op=ALU.is_equal, fill=-BIG, base=0,
                             pattern=[[-1, NE], [0, H]], channel_multiplier=1).then_inc(s_c, 1)

            def gather(it, j, first):
                for hf in range(2):
                    if not first:
                        for k in range(UN // 2):
                            gp.wait_ge(g_in[hf * UN // 2 + k], it * 16)
                    gp.tensor_copy(ixb[:, hf, :], dst_i[:, bass.ds(j * UN + hf * (UN // 2), UN // 2)]).then_inc(p_ix, 1)
                    gp.wait_ge(p_ix, it * 2 + hf + 1)
                    for k in range(UN // 2):
                        kk = hf * (UN // 2) + k
                        if not first:
                            gp.wait_ge(pe_e, it * UN - (UN - kk - 1))
                        gp.sem_inc(alone_gp, 1)
                        gp.indirect_dma_start(grow[:, kk, 0:D], None, y_table,
                                              bass.IndirectOffsetOnAxis(ap=ixb[:, hf, k:k + 1], axis=0)
                                              ).then_inc(g_in[kk], 16)

            STEPS = EC // UN
            gather(0, 0, True)
            with gp.Fori(1, STEPS) as j:
                gather(j, j, False)
            with gp.Fori(1, NS // PASS) as r:
                with gp.Fori(0, STEPS) as j:
                    gather(r * STEPS + j, j, False)
            with gp.Fori(0, G) as g:
                for t in range(2):
                    gp.wait_ge(f_ag, g * 2 + t + 1)
                    gp.sem_inc(alone_gp, 1)
                    gp.tensor_scalar(ve[:, t:t + 1], fmv[:, t, 1:2], EPS, None, ALU.add).then_inc(p_ve, 1)
                    gp.wait_ge(p_ve, g * 2 + t + 1 + NS)
                    gp.tensor_tensor(frs[:, t:t + 1], ve[:, t:t + 1], mhalf[0:NB], ALU.pow).then_inc(f_rs, 1)

        @block.scalar
        def _(act):
            act.wait_ge(s_id, 8)

            def xt_copy(s, par):
                act.wait_ge(pe_tr, s + 1)
                wait(act, pe_yz, s - 1)
                act.copy(xt[:, par], ps[:, par, 0:250].rearrange("p (c n) -> p c n", c=2)).then_inc(a_xt, 1)
                act.copy(xnT[:, :, bass.ds(s * NB, NB)], ps[:, par, 0:250].rearrange("p (c n) -> p c n", c=2)).then_inc(a_xt2, 1)

            def kv_act(s, par):
                act.wait_ge(pe_kv, s + 1)
                wait(act, pe_cx, s - 1)
                act.copy(vv[:, par].rearrange("p (c n) -> p c n", c=2)[:, :, 0:128],
                         ps[0:NB, 2 + par, 256:512].rearrange("p (c n) -> p c n", c=2)).then_inc(a_v, 1)
                act.wait_ge(pe_yz, s + 1)
                act.copy(agg_sb[:, s, 0:D], ps[0:NB, 4 + par, 0:D]).then_inc(a_y, 1)
                act.wait_ge(v_km, s + 1)
                wait(act, v_kf, s - 1)
                act.activation(kx[:, par], km[:, par], ACT.Exp).then_inc(a_kx, 1)

            run(act, NS, [(0, xt_copy), (1, kv_act)])

            def q_exp(g, par):
                act.wait_ge(v_qm, g + 1)
                wait(act, v_qf, g - 1)
                act.activation(qx[par], qm[par], ACT.Exp).then_inc(a_qx, 1)

            run(act, G, [(0, q_exp)])
            act.wait_ge(s_f, 112)

            def xf_copy(g, par):
                act.wait_ge(f_tr, g + 1)
                act.wait_ge(f_h, g * JH)
                act.wait_ge(f_lg, g * 2)
                act.copy(xfT[:].rearrange("p c t n -> p (c t n)"), ps[:, 0, 0:500]).then_inc(f_xt, 1)
                act.wait_ge(f_ot, g + 1)
                act.copy(oeT[:].rearrange("p t n -> p (t n)"), ps[0:NE, 1, 0:250]).then_inc(f_os, 1)
                act.wait_ge(f_o, g * 2)
                for j in range(JH):
                    act.wait_ge(f_h, g * JH + j + 1)
                    act.activation(hs[:, j, :], ps[:, 2 + j % 2, 0:250], ACT.Relu, bias=b1_sb[:, j:j + 1]).then_inc(f_hs, 1)

            with act.Fori(0, G) as g:
                xf_copy(g, 0)

        @block.tensor
        def _(pe):
            pe.wait_ge(s_id, 8)
            pe.wait_ge(s_w, 80)

            def tr(s, par):
                pe.wait_ge(v_xn, s + 1)
                wait(pe, a_xt2, s - 1)
                for c in range(2):
                    mm = pe.transpose(ps[:, par, c * NB:(c + 1) * NB], xn[:, par, c * 128:(c + 1) * 128], ident[0:NB, 0:NB])
                mm.then_inc(pe_tr, 1)

            def kvyz(s, par):
                pe.wait_ge(a_xt, s + 1)
                wait(pe, v_kf, s - 1)
                wait(pe, a_v, s - 1)
                for c in range(2):
                    mm = pe.matmul(ps[0:NB, 2 + par, :], xt[:, par, c, :], wkv_sb[:, c, :], start=(c == 0), stop=(c == 1))
                mm.then_inc(pe_kv, 1)
                wait(pe, a_y, s - 1)
                wait(pe, v_base, s - 1)
                for c in range(2):
                    mm = pe.matmul(ps[0:NB, 4 + par, :], xt[:, par, c, :], wyz_sb[:, c, :], start=(c == 0), stop=(c == 1))
                mm.then_inc(pe_yz, 1)

            def context(s, par):
                pe.wait_ge(v_kf, s + 1)
                pe.wait_ge(a_v, s + 1)
                for c in range(2):
                    mm = pe.matmul(ps[:, 6 + c, 0:129], kf[:, par, c * 128:(c + 1) * 128], vv[:, par, c * 129:(c + 1) * 129],
                                   start=False, stop=False, skip_group_check=True) if not (isinstance(s, int) and s in (0, NS - 1)) else \
                        pe.matmul(ps[:, 6 + c, 0:129], kf[:, par, c * 128:(c + 1) * 128], vv[:, par, c * 129:(c + 1) * 129],
                                  start=(s == 0), stop=(s == NS - 1), skip_group_check=True)
                mm.then_inc(pe_cx, 1)

            run(pe, NS, [(0, tr), (1, kvyz), (2, context)])
            pe.wait_ge(v_cm, 4)
            for c in range(2):
                mm = pe.transpose(ps[:, 0, c * 128:(c + 1) * 128], cbd[:, c, :], ident[:])
            mm.then_inc(pe_ct, 1)
            pe.wait_ge(v_ct, 1)
            for c in range(2):
                mm = pe.matmul(ps[:, 1, c * 256:(c + 1) * 256], cbdT[:, c, :], wp_sb[:, c, :], start=True, stop=True)
            mm.then_inc(pe_m, 1)

            def q(g, par):
                wait(pe, v_qf, g - 1)
                if isinstance(g, int) and g < 2:
                    pe.wait_ge(v_m, 1)
                    pe.wait_ge(a_xt2, NS)
                for o in range(2):
                    for c in range(2):
                        mm = pe.matmul(ps[:, 2 + par, o * 250:(o + 1) * 250], wq_sb[:, c, o * 128:(o + 1) * 128],
                                       xnT[:, c, bass.ds(g * 250, 250)], start=(c == 0), stop=(c == 1))
                mm.then_inc(pe_q, 1)

            def den(g, par):
                pe.wait_ge(v_qf, g + 1)
                wait(pe, v_dn, g - 1)
                for o in range(2):
                    mm = pe.matmul(ps[:, 4 + par, o * 250:(o + 1) * 250], ksb[:, o, :], qf[par][:, o * 250:(o + 1) * 250],
                                   start=True, stop=True)
                mm.then_inc(pe_dn, 1)

            def att(g, par):
                pe.wait_ge(v_qs, g + 1)
                wait(pe, v_at, g - 1)
                for t in range(2):
                    for o in range(2):
                        mm = pe.matmul(ps[0:NB, 6 + par, t * 256:(t + 1) * 256],
                                       qs[par][:, o * 250 + t * NB:o * 250 + (t + 1) * NB], msb[:, o, :],
                                       start=(o == 0), stop=(o == 1))
                mm.then_inc(pe_at, 1)

            run(pe, G, [(0, q), (1, den), (2, att)])
            pe.wait_ge(v_at, G)

            def edges(it, first, last):
                for k in range(UN):
                    pe.wait_ge(g_in[k], it * 16 + 16)
                    pe.wait_ge(v_oh, it * UN + k + 1)
                    for c in range(PASS):
                        mm = pe.matmul(ps[0:NB, c, 0:D + 1], oneh[:, k % 2, c * NB:(c + 1) * NB], grow[:, k, :],
                                       start=(first and k == 0), stop=(last and k == UN - 1), skip_group_check=True)
                    mm.then_inc(pe_e, 1)

            STEPS = EC // UN
            with pe.Fori(0, NS // PASS) as r:
                pe.wait_ge(v_agg, r)
                edges(r * STEPS, True, False)
                with pe.Fori(1, STEPS - 1) as j:
                    edges(r * STEPS + j, False, False)
                edges(r * STEPS + (STEPS - 1), False, True)

            pe.wait_ge(v_agg, NS // PASS)
            pe.wait_ge(s_c, 3)
            pe.wait_ge(s_f, 112)

            def ffn(g):
                pe.wait_ge(f_xf, g * 2 + 2)
                for c in range(2):
                    for t in range(2):
                        mm = pe.transpose(ps[:, 0, c * 250 + t * NB:c * 250 + (t + 1) * NB], fxf[:, t, c * 128:(c + 1) * 128],
                                          ident[0:NB, 0:NB])
                mm.then_inc(f_tr, 1)
                pe.wait_ge(f_xt, g + 1)
                for t in range(2):
                    for c in range(2):
                        mm = pe.matmul(ps[0:NB, 1, t * NE:(t + 1) * NE], xfT[:, c, t, :], rw_sb[:, c, :], start=(c == 0), stop=(c == 1))
                    mm.then_inc(f_lg, 1)
                pe.wait_ge(f_oh, g * 2 + 2)
                for t in range(2):
                    mm = pe.transpose(ps[0:NE, 1, t * NB:(t + 1) * NB], oe[:, t, :], ident[0:NB, 0:NB])
                mm.then_inc(f_ot, 1)
                pe.wait_ge(f_os, g + 1)
                for j in range(JH):
                    wait(pe, f_hs, g * JH + j - 1) if j else None
                    for c in range(2):
                        pe.matmul(ps[:, 2 + j % 2, 0:250], w1_sb[:, c, j * 128:(j + 1) * 128],
                                  xfT[:, c].rearrange("p t n -> p (t n)"), start=(c == 0), stop=False)
                    pe.matmul(ps[:, 2 + j % 2, 0:250], off0[:, j * 128:(j + 1) * 128], oeT[:].rearrange("p t n -> p (t n)"),
                              start=False, stop=True).then_inc(f_h, 1)
                pe.wait_ge(f_hs, g * JH + JH)
                pe.wait_ge(f_r, g * 2)
                for t in range(2):
                    for j in range(JH):
                        pe.matmul(ps[0:NB, 4 + t, 0:D], hs[:, j, t * NB:(t + 1) * NB], w2_sb[:, j, :], start=(j == 0), stop=False)
                    pe.matmul(ps[0:NB, 4 + t, 0:D], oeT[:, t, :], b2_sb[:], start=False, stop=True).then_inc(f_o, 1)

            with pe.Fori(0, G) as g:
                ffn(g)

        @block.vector
        def _(v):
            v.memset(src_i[:], -1).then_inc(v_e, 1)
            v.memset(dst_i[:], 0).then_inc(v_e, 1)
            v.wait_ge(s_w, 80)
            v.tensor_tensor(biast[:], bias_sb[:, 0], bias_sb[:, 1], ALU.add).then_inc(v_bias, 1)
            v.wait_ge(v_bias, 1)
            v.tensor_tensor(bias[:], biast[:], bias_sb[:, 2], ALU.add).then_inc(v_bias, 1)
            v.wait_ge(s_in, 32)

            def norm(s, par):
                wait(v, v_rs, s - 1)
                v.sem_inc(alone_v, 1)
                v.bn_stats(st[:, par], x_sb[:, s, :]).then_inc(v_st, 1)
                v.wait_ge(v_st, s + 1)
                v.sem_inc(alone_v, 1)
                v.bn_aggr(mv[:, par], st[:, par]).then_inc(v_ag, 1)
                v.wait_ge(v_ag, s + 1)
                v.wait_ge(v_rs, s + 1)
                wait(v, pe_tr, s - 1)
                v.tensor_scalar(xn[:, par], x_sb[:, s, :], mv[:, par, 0:1], rs[:, par:par + 1], ALU.subtract, ALU.mult).then_inc(v_xn, 1)

            def kv_dve(s, par):
                v.wait_ge(a_v, s + 1)
                wait(v, a_kx, s - 1)
                v.tensor_scalar(km[:, par], ps[0:NB, 2 + par, 0:256], 0.0, None, ALU.min).then_inc(v_km, 1)
                v.wait_ge(a_y, s + 1)
                v.wait_ge(p_b, s + 1)
                v.tensor_tensor(x_sb[:, s, :], x_sb[:, s, :], ps[0:NB, 4 + par, 256:512], ALU.add).then_inc(v_base, 1)
                v.wait_ge(a_kx, s + 1)
                wait(v, pe_cx, s - 1)
                v.scalar_tensor_tensor(kf[:, par], ps[0:NB, 2 + par, 0:256], 0.0, kx[:, par], ALU.max, ALU.add).then_inc(v_kf, 1)

            run(v, NS, [(0, norm), (1, kv_dve)])
            v.wait_ge(pe_cx, NS)
            v.wait_ge(s_id, 8)
            for c in range(2):
                v.tensor_copy(cx[:, c], ps[:, 6 + c, 0:129]).then_inc(v_cx, 1)
            v.wait_ge(v_cx, 2)
            for c in range(2):
                v.tensor_tensor(cbd[:, c], cx[:, c, 0:128], hmask[:], ALU.mult).then_inc(v_cm, 1)
                v.tensor_scalar(ksb[:, c], hmask[:], cx[:, c, 128:129], None, ALU.mult).then_inc(v_cm, 1)
            v.wait_ge(pe_ct, 1)
            v.tensor_copy(cbdT[:].rearrange("p c n -> p (c n)"), ps[:, 0, 0:256]).then_inc(v_ct, 1)
            v.wait_ge(pe_m, 1)
            v.tensor_copy(msb[:].rearrange("p c n -> p (c n)"), ps[:, 1, :]).then_inc(v_m, 1)

            def q_min(g, par):
                v.wait_ge(pe_q, g + 1)
                wait(v, a_qx, g - 1)
                v.tensor_scalar(qm[par], ps[:, 2 + par, 0:500], 0.0, None, ALU.min).then_inc(v_qm, 1)
                v.wait_ge(a_qx, g + 1)
                wait(v, pe_dn, g - 1)
                v.scalar_tensor_tensor(qf[par], ps[:, 2 + par, 0:500], 0.0, qx[par], ALU.max, ALU.add).then_inc(v_qf, 1)

            def q_scale(g, par):
                v.wait_ge(pe_dn, g + 1)
                v.tensor_scalar(dn[par], ps[:, 4 + par, 0:500], 1e-6, None, ALU.max).then_inc(v_dn, 1)
                v.wait_ge(v_dn, g + 1)
                v.reciprocal(qm2[par], dn[par]).then_inc(v_rc, 1)
                v.wait_ge(v_rc, g + 1)
                wait(v, pe_at, g - 1)
                v.tensor_tensor(qs[par], qf[par], qm2[par], ALU.mult).then_inc(v_qs, 1)

            def base(g, par):
                v.wait_ge(pe_at, g + 1)
                v.tensor_tensor(x_sb[:, bass.ds(g * 2, 2), :], x_sb[:, bass.ds(g * 2, 2), :],
                                ps[0:NB, 6 + par, :].rearrange("p (t d) -> p t d", t=2), ALU.add).then_inc(v_at, 1)

            run(v, G, [(0, q_min), (1, q_scale), (2, base)])
            v.wait_ge(s_e, 64)
            v.tensor_copy(srcf[:], src_i[:]).then_inc(v_sub, 1)
            v.wait_ge(v_at, G)
            v.wait_ge(v_sub, 1)
            v.wait_ge(y_out, 160)

            STEPS = EC // UN

            def hot(it, j, first):
                for k in range(UN):
                    if not (first and k < 2):
                        v.wait_ge(pe_e, it * UN + k - 1)
                    v.tensor_scalar(oneh[:, k % 2], nodes[:].rearrange("p a b -> p (a b)"),
                                    srcf[:, bass.ds(j * UN + k, 1)], None, ALU.is_equal).then_inc(v_oh, 1)

            with v.Fori(0, NS // PASS) as r:
                v.wait_ge(v_sub, r + 1)
                for k in range(2):
                    v.wait_ge(pe_e, r * STEPS * UN)
                    v.tensor_scalar(oneh[:, k], nodes[:].rearrange("p a b -> p (a b)"), srcf[:, k:k + 1], None, ALU.is_equal).then_inc(v_oh, 1)
                for k in range(2, UN):
                    v.wait_ge(pe_e, r * STEPS * UN + (k - 1))
                    v.tensor_scalar(oneh[:, k % 2], nodes[:].rearrange("p a b -> p (a b)"), srcf[:, k:k + 1], None, ALU.is_equal).then_inc(v_oh, 1)
                with v.Fori(1, STEPS) as j:
                    hot(r * STEPS + j, j, False)
                v.wait_ge(pe_e, r * STEPS * UN + STEPS * UN)
                v.tensor_copy(agg_sb[:, bass.ds(r * PASS, PASS), :], ps[0:NB, 0:PASS, 0:D + 1]).then_inc(v_agg, 1)
                v.wait_ge(v_oh, r * STEPS * UN + STEPS * UN)
                v.tensor_scalar(srcf[:], srcf[:], -float(PASS), None, ALU.add).then_inc(v_sub, 1)

            v.wait_ge(v_agg, NS // PASS)
            v.tensor_scalar(rc0[:], agg_sb[:, :, D], 1.0, None, ALU.max).then_inc(f_rc, 1)
            v.wait_ge(f_rc, 1)
            v.reciprocal(rc[:], rc0[:]).then_inc(f_rc, 1)
            v.wait_ge(f_rc, 2)
            v.wait_ge(s_f, 112)

            with v.Fori(0, G) as g:
                for t in range(2):
                    s = g * 2 + t
                    v.scalar_tensor_tensor(x_sb[:, s, :], agg_sb[:, s, 0:D], rc[:, bass.ds(s, 1)], x_sb[:, s, :], ALU.mult, ALU.add).then_inc(f_x1, 1)
                    v.wait_ge(f_x1, s + 1)
                    v.sem_inc(alone_v, 1)
                    v.bn_stats(fst[:, t], x_sb[:, s, :]).then_inc(f_st, 1)
                    v.wait_ge(f_st, s + 1)
                    v.sem_inc(alone_v, 1)
                    v.bn_aggr(fmv[:, t], fst[:, t]).then_inc(f_ag, 1)
                    v.wait_ge(f_ag, s + 1)
                    v.wait_ge(f_rs, s + 1)
                    v.wait_ge(f_tr, g)
                    v.tensor_scalar(fxf[:, t], x_sb[:, s, :], fmv[:, t, 0:1], frs[:, t:t + 1], ALU.subtract, ALU.mult).then_inc(f_xf, 1)
                for t in range(2):
                    s = g * 2 + t
                    v.wait_ge(f_lg, g * 2 + 2)
                    v.tensor_tensor(lg[:, t], ps[0:NB, 1, t * NE:(t + 1) * NE], rb_sb[0:NB], ALU.add).then_inc(f_lb, 1)
                    v.wait_ge(f_lb, s + 1)
                    v.sem_inc(alone_v, 1)
                    v.max(mx[:, t], lg[:, t]).then_inc(f_mx, 1)
                    v.wait_ge(f_mx, s + 1)
                    v.sem_inc(alone_v, 1)
                    v.max_index(mi[:, t], mx[:, t], lg[:, t]).then_inc(f_ix, 1)
                    v.wait_ge(f_ix, s + 1)
                    v.tensor_copy(mf[:, t], mi[:, t, 0:1]).then_inc(f_if, 1)
                    v.wait_ge(f_if, s + 1)
                    v.wait_ge(f_ot, g)
                    v.tensor_scalar(oe[:, t], iota_e[0:NB], mf[:, t], None, ALU.is_equal).then_inc(f_oh, 1)
                for t in range(2):
                    s = g * 2 + t
                    v.wait_ge(f_o, s + 1)
                    v.scalar_tensor_tensor(x_sb[:, s, :], ps[0:NB, 4 + t, 0:D], 0.0, x_sb[:, s, :], ALU.max, ALU.add).then_inc(f_y, 1)
                v.wait_ge(f_y, g * 2 + 2)
                v.nop().then_inc(f_r, 2)


_OUT = ((N, D), "float32")


def kernel(**inputs):
    import numpy as np
    import concourse.bacc as bacc
    from concourse.bass_utils import run_bass_kernel_spmd as launch

    a = {k: np.asarray(v) for k, v in inputs.items()}
    lay = {
        "x": a["x"], "src": a["src"], "dst": a["dst"],
        "wkv": a["L0_mix_Wkv"].T, "wyz": np.concatenate([a["L0_gnn_W2"].T, a["L0_gnn_W1"].T], 1),
        "wq": a["L0_mix_Wq"].T, "wproj": a["L0_mix_Wproj"].T,
        "bias3": np.stack([a["L0_gnn_b1"], a["L0_gnn_b2"], a["L0_mix_bproj"]]),
        "rw": a["L0_ffn_router_w"].T, "rb": a["L0_ffn_router_b"],
        "w1": a["L0_ffn_W1"], "b1": a["L0_ffn_b1"].reshape(JH, 128).T,
        "w2": a["L0_ffn_W2"].reshape(NE * H, D), "b2": a["L0_ffn_b2"],
    }
    nc = bacc.Bacc("TRN2", target_bir_lowering=False, num_devices=1)
    arrays, args = {}, []
    for name, v in lay.items():
        v = np.ascontiguousarray(v)
        arrays[f"in_{name}"] = v
        args.append(nc.dram_tensor(f"in_{name}", v.shape, mybir.dt.from_np(v.dtype), kind="ExternalInput").ap())
    args.append(nc.dram_tensor("out_0", _OUT[0], F32, kind="ExternalOutput").ap())
    gps_layer(nc, *args)
    r = launch(nc, [arrays], core_ids=[0])
    return r.results[0]["out_0"]
```

```python
from contextlib import ExitStack

import concourse.bass as bass
from concourse import mybir

ALU = mybir.AluOpType
ACT = mybir.ActivationFunctionType
F32 = mybir.dt.float32
I32 = mybir.dt.int32
U32 = mybir.dt.uint32

N, D = 6250, 256
NB, NS = 125, 50
E = 106250
GC = 15
NG = 56
GE = 128 * GC
EC = NG * GC
NI = NS // 2
NW = NI * GC
QP = NG // 2
RING = 4
HEADS, DH = 8, 32
NE, H = 32, 64
JH = NE * H // 128
G = NS // 2
PASS = 5
UN = 8
EPS = 1e-5
BIG = 1e30
BF16 = mybir.dt.bfloat16
F32R = mybir.dt.float32r


def wait(eng, sem, value):
    if isinstance(value, int) and value <= 0:
        return
    eng.wait_ge(sem, value)


def run(eng, n, stages, peel=4):
    lag = max(l for l, _ in stages)
    half = (n - peel) // 2

    def static(step):
        for l, work in stages:
            if 0 <= step - l < n:
                work(step - l, (step - l) % 2)

    for step in range(peel):
        static(step)
    with eng.Fori(0, half) as i:
        for u in range(2):
            for l, work in stages:
                work(i * 2 + (peel + u - l), (peel + u - l) % 2)
    for step in range(peel + 2 * half, n + lag):
        static(step)


def gps_layer(nc, x, src, dst, wkv, wyz, wq, wproj, bias3, rw, rb, w1, b1, w2, b2, out):
    y_table = nc.dram_tensor("y_table", [N, D], F32).ap()
    with ExitStack() as ctx:
        def sb(name, shape, dt=F32):
            return ctx.enter_context(nc.sbuf_tensor(name, shape, dt))

        def sem(name):
            return ctx.enter_context(nc.semaphore(name))

        ps = ctx.enter_context(nc.psum_tensor("ps", [128, 8, 512], F32))

        x_sb = sb("x_sb", [NB, NS, D])
        routed = sb("routed", [128, 2, NI, NG])
        ident = sb("ident", [128, 128])
        mhalf = sb("mhalf", [128, 1])
        iota_b = sb("iota_b", [128, 256], BF16)
        window_ix = sb("window_ix", [128, NG], U32)
        fits = sb("fits", [1, 1], I32)

        phase = ExitStack()

        def pb(name, shape, dt=F32):
            return phase.enter_context(nc.sbuf_tensor(name, shape, dt))[:]

        src_i = pb("src_i", [128, EC], I32)
        dst_i = pb("dst_i", [128, EC], I32)
        sf, df, tf = pb("sf", [128, EC]), pb("df", [128, EC]), pb("tf", [128, EC])
        bi = pb("bi", [128, EC], I32)
        bf, tile_f, blk, vs, vd = (pb(n, [128, EC]) for n in ("bf", "tile_f", "blk", "vs", "vd"))
        valid = pb("valid", [128, EC])
        base_f = pb("base_f", [128, NG])
        pcol = pb("pcol", [128, 1])
        win_f = pb("win_f", [128, NG])
        iota_i = pb("iota_i", [128, NI])
        iota_r = pb("iota_r", [128, 128], BF16)
        restart = pb("restart", [128, NW], BF16)
        before = pb("before", [128, 128], BF16)
        ident_b = pb("ident_b", [128, 128], BF16)
        ones_f = pb("ones_f", [128, 128])
        ohI = [pb(f"ohI{k}", [128, NW], BF16) for k in range(2)]
        pre = [pb(f"pre{k}", [128, NW], BF16) for k in range(2)]
        prod = [pb(f"prod{k}", [128, NW]) for k in range(2)]
        vals = [pb(f"vals{k}", [128, GC, 2, NI], BF16) for k in range(2)]
        ohr = [pb(f"ohr{k}", [128, GC, 128], BF16) for k in range(2)]
        rank = pb("rank", [128, EC])
        top = pb("top", [128, 4])
        good = pb("good", [128, 4])
        phase.close()

        agg_sb = pb("agg_sb", [NB, NS, D + 1])
        xnT = pb("xnT", [128, 2, N])
        wkv_sb = pb("wkv_sb", [128, 2, 2 * D])
        wyz_sb = pb("wyz_sb", [128, 2, 2 * D])
        wq_sb = pb("wq_sb", [128, 2, D])
        wp_sb = pb("wp_sb", [128, 2, D])
        bias_sb = pb("bias_sb", [128, 3, D])
        bias = pb("bias", [128, D])
        biast = pb("biast", [128, D])
        st = pb("st", [NB, 2, 6])
        mv = pb("mv", [NB, 2, 2])
        rs = pb("rs", [NB, 2])
        ve = pb("ve", [NB, 2])
        xn = pb("xn", [NB, 2, D])
        xt = pb("xt", [128, 2, 2, NB])
        km = pb("km", [NB, 2, D])
        kx = km
        kf = pb("kf", [NB, 2, D])
        vv = pb("vv", [NB, 2, D + 2])
        cx = pb("cx", [128, 2, 129])
        cbd = pb("cbd", [128, 2, 128])
        cbdT = pb("cbdT", [128, 2, 128])
        hmask = pb("hmask", [128, 128])
        hm0 = pb("hm0", [128, 128])
        ksb = pb("ksb", [128, 2, 128])
        msb = pb("msb", [128, 2, D])
        qm = [pb(f"qm{k}", [128, 500])[:] for k in range(2)]
        qx = qm
        dn = [pb(f"dn{k}", [128, 500])[:] for k in range(2)]
        qm2 = dn
        qf = [pb(f"qf{k}", [128, 500])[:] for k in range(2)]
        qs = [wkv_sb[:, k, 0:500] for k in range(2)]
        phase.close()

        y_hi = pb("y_hi", [128, NG, D + 2], F32R)
        y_lo = pb("y_lo", [128, NG, D], F32R)
        raw = pb("raw", [128, 4, D])
        wix = pb("wix", [128, 2, 4], U32)
        cnt_T = [pb(f"cnt_T{k}", [128, 2, 2, 128], F32R) for k in range(2)]
        oht = pb("oht", [128, RING, 2, 128], BF16)
        ohs = pb("ohs", [128, RING, 2, 256], BF16)
        cm = pb("cm", [NB, 2])
        cr = pb("cr", [NB, 2])
        phase.close()

        agg2 = pb("agg2", [NB, NS, D + 1])
        src2 = pb("src2", [128, EC], I32)
        dst2 = pb("dst2", [128, EC], I32)
        srcf = pb("srcf", [128, EC])
        nodes = pb("nodes", [128, PASS, NB])
        ixb = pb("ixb", [128, 2, UN // 2], U32)
        grow = pb("grow", [128, UN, D + 1])
        oneh = pb("oneh", [128, 2, PASS * NB])
        rc = pb("rc", [NB, NS])
        rc0 = pb("rc0", [NB, NS])
        phase.close()

        w1_sb = pb("w1_sb", [128, 2, NE * H])
        w2_sb = pb("w2_sb", [128, JH, D])
        hs = pb("hs", [128, JH, 250])
        off0 = pb("off0", [NE, NE * H])
        rw_sb = pb("rw_sb", [128, 2, NE])
        rb_sb = pb("rb_sb", [128, NE])
        b1_sb = pb("b1_sb", [128, JH])
        b2_sb = pb("b2_sb", [NE, D])
        iota_e = pb("iota_e", [128, NE])
        xfT = pb("xfT", [128, 2, 2, NB])
        lg = pb("lg", [NB, 2, NE])
        mx = pb("mx", [NB, 2, 8])
        mi = pb("mi", [NB, 2, 8], U32)
        mf = pb("mf", [NB, 2, 1])
        oe = pb("oe", [NB, 2, NE])
        oeT = pb("oeT", [NE, 2, NB])
        fst = pb("fst", [NB, 2, 6])
        fmv = pb("fmv", [NB, 2, 2])
        frs = pb("frs", [NB, 2])
        fve = pb("fve", [NB, 2])
        fxf = pb("fxf", [NB, 2, D])
        phase.close()

        s_in, s_w, s_id, s_c = sem("s_in"), sem("s_w"), sem("s_id"), sem("s_c")
        v_bias, v_st, v_ag, v_rs, v_xn = sem("v_bias"), sem("v_st"), sem("v_ag"), sem("v_rs"), sem("v_xn")
        p_b, pe_tr, a_xt, a_xt2, pe_kv, pe_yz = sem("p_b"), sem("pe_tr"), sem("a_xt"), sem("a_xt2"), sem("pe_kv"), sem("pe_yz")
        v_km, a_kx, v_kf, a_v, a_y, v_base, pe_cx = (sem(n) for n in ("v_km", "a_kx", "v_kf", "a_v", "a_y", "v_base", "pe_cx"))
        y_out, v_cx, v_bd, pe_ct, v_ct, pe_m, v_m = (sem(n) for n in ("y_out", "v_cx", "v_bd", "pe_ct", "v_ct", "pe_m", "v_m"))
        pe_q, v_qm, a_qx, v_qf, pe_dn, v_dn, v_rc, v_qs, pe_at, v_at = (sem(n) for n in (
            "pe_q", "v_qm", "a_qx", "v_qf", "pe_dn", "v_dn", "v_rc", "v_qs", "pe_at", "v_at"))
        s_e, v_e, p_ix, p_z, v_sub, v_oh, pe_e, pe_pass, v_agg = (sem(n) for n in (
            "s_e", "v_e", "p_ix", "p_z", "v_sub", "v_oh", "pe_e", "pe_pass", "v_agg"))
        g_in = [sem(f"g_in{k}") for k in range(UN)]
        s_f, p_ve, p_k = sem("s_f"), sem("p_ve"), sem("p_k")
        f_c, f_rc, f_x1, f_st, f_ag, f_rs, f_xf = (sem(n) for n in ("f_c", "f_rc", "f_x1", "f_st", "f_ag", "f_rs", "f_xf"))
        f_tr, f_xt, f_lg, f_lb, f_mx, f_ix, f_if, f_oh, f_ot, f_os, f_h, f_hs, f_o, f_r, f_y = (sem(n) for n in (
            "f_tr", "f_xt", "f_lg", "f_lb", "f_mx", "f_ix", "f_if", "f_oh", "f_ot", "f_os", "f_h", "f_hs", "f_o", "f_r", "f_y"))
        f_out = sem("f_out")
        alone_v, alone_gp = sem("alone_v"), sem("alone_gp")

        r_ld, r_pad, r_v, pe_base, r_fit, pe_fit = (sem(n) for n in ("r_ld", "r_pad", "r_v", "pe_base", "r_fit", "pe_fit"))
        r_oh, r_pre, pe_rk, r_prod, r_r, r_ohr, p_val, pe_rt, a_rv, r_ready = (sem(n) for n in (
            "r_oh", "r_pre", "pe_rk", "r_prod", "r_r", "r_ohr", "p_val", "pe_rt", "a_rv", "r_ready"))
        w_ix, a_hi, v_lo, v_o, pe_a, a_cn, pe_d, v_cm, v_cr, v_ev, x1_ready = (sem(n) for n in (
            "w_ix", "a_hi", "v_lo", "v_o", "pe_a", "a_cn", "pe_d", "w_cm", "w_cr", "v_ev", "x1_ready"))
        p_one, b_rc, b_x1, q_c = sem("p_one"), sem("b_rc"), sem("b_x1"), sem("q_c")
        w_in = [sem(f"w_in{k}") for k in range(4)]

        x_v = x.rearrange("(b s) d -> b s d", s=NS)
        y_v = y_table.rearrange("(b s) d -> b s d", s=NS)
        o_v = out.rearrange("(b s) d -> b s d", s=NS)
        HALVES = ((0, 112), (112, NB))

        block = ctx.enter_context(nc.Block())

        def load_edges(eng, t_src, t_dst, done):
            last = E - (NG - 1) * GE
            rows = last // GC
            for t, w in ((t_src, src), (t_dst, dst)):
                eng.dma_start(t[:, 0:(NG - 1) * GC].rearrange("p (g c) -> p g c", c=GC),
                              w[0:(NG - 1) * GE].rearrange("(g p c) -> p g c", p=128, c=GC)).then_inc(done, 16)
                eng.dma_start(t[0:rows, (NG - 1) * GC:EC],
                              w[(NG - 1) * GE:(NG - 1) * GE + rows * GC].rearrange("(p c) -> p c", c=GC)).then_inc(done, 16)
                eng.dma_start(t[rows:rows + 1, (NG - 1) * GC:(NG - 1) * GC + last - rows * GC],
                              w[(NG - 1) * GE + rows * GC:E].rearrange("(p c) -> p c", p=1)).then_inc(done, 16)

        @block.sync
        def _(sp):
            sp.wait_ge(r_pad, 2)
            load_edges(sp, src_i, dst_i, r_ld)
            for a, b in HALVES:
                sp.dma_start(x_sb[a:b], x_v[a:b]).then_inc(s_in, 16)
            sp.wait_ge(r_fit, 1)
            sp.wait_ge(a_rv, NG)
            for k, (t, w) in enumerate(((wkv_sb, wkv), (wyz_sb, wyz), (wq_sb, wq), (wp_sb, wproj))):
                sp.dma_start(t[:], w.rearrange("(c p) o -> p c o", p=128)).then_inc(s_w, 16)
            sp.dma_start(bias_sb[:], bias3.rearrange("a d -> () a d").to_broadcast([128, 3, D])).then_inc(s_w, 16)
            for k in range(5):
                sp.wait_ge(a_y, 10 * (k + 1))
                for a, b in HALVES:
                    sp.dma_start(y_v[a:b, 10 * k:10 * k + 10], agg_sb[a:b, 10 * k:10 * k + 10, 0:D]).then_inc(y_out, 16)
            sp.wait_ge(x1_ready, 1)
            for c in range(2):
                sp.dma_start(w1_sb[:, c].rearrange("p (e h) -> p e h", e=NE),
                             w1[:, c * 128:(c + 1) * 128].rearrange("e p h -> p e h")).then_inc(s_f, 16)
            sp.dma_start(w2_sb, w2.rearrange("(j p) d -> p j d", p=128)).then_inc(s_f, 16)
            sp.dma_start(rw_sb[:], rw.rearrange("(c p) o -> p c o", p=128)).then_inc(s_f, 16)
            sp.dma_start(rb_sb[:], rb.rearrange("n -> () n").to_broadcast([128, NE])).then_inc(s_f, 16)
            sp.dma_start(b1_sb[:], b1).then_inc(s_f, 16)
            sp.dma_start(b2_sb[:], b2).then_inc(s_f, 16)
            for k in range(5):
                sp.wait_ge(f_y, 10 * (k + 1))
                for a, b in HALVES:
                    sp.dma_start(o_v[a:b, 10 * k:10 * k + 10], x_sb[a:b, 10 * k:10 * k + 10]).then_inc(f_out, 16)
            sp.wait_ge(f_out, 160)

        @block.gpsimd
        def _(gp):
            gp.memset(src_i[:], -1).then_inc(r_pad, 1)
            gp.memset(dst_i[:], 0).then_inc(r_pad, 1)
            gp.memset(ident[:], 0.0).then_inc(q_c, 1)
            gp.memset(ident_b[:], 0.0).then_inc(q_c, 1)
            gp.memset(before[:], 1.0).then_inc(q_c, 1)
            gp.memset(ones_f[:], 1.0).then_inc(q_c, 1)
            gp.memset(restart[:], 1.0).then_inc(q_c, 1)
            gp.memset(mhalf[:], -0.5).then_inc(q_c, 1)
            gp.wait_ge(q_c, 6)
            for m in (ident, ident_b):
                gp.affine_select(out=m[:], in_=m[:], compare_op=ALU.not_equal, fill=1.0, base=0,
                                 pattern=[[-1, 128]], channel_multiplier=1).then_inc(q_c, 1)
            gp.affine_select(out=before[:], in_=before[:], compare_op=ALU.is_gt, fill=0.0, base=0,
                             pattern=[[1, 128]], channel_multiplier=-1).then_inc(q_c, 1)
            gp.memset(restart[:].rearrange("p (i c) -> p i c", c=GC)[:, :, 0:1], 0.0).then_inc(q_c, 1)
            for t, pattern, base, mult in ((iota_b, [[1, 256]], 1, 0), (iota_r, [[1, 128]], 0, 0),
                                           (iota_i, [[1, NI]], 0, 0), (pcol, [[1, 1]], 0, 1)):
                gp.iota(t[:], pattern, base=base, channel_multiplier=mult, allow_small_or_imprecise_dtypes=True).then_inc(q_c, 1)

            def values(g, par):
                gp.wait_ge(r_oh, g + 1)
                wait(gp, pe_rt, g - 1)
                hot = ohI[par][:].rearrange("p (i c) -> p c i", c=GC)
                for k, t in enumerate((vd, vs)):
                    col = t[:, bass.ds(g * GC, GC)].rearrange("p (c a) -> p c a", a=1).to_broadcast([128, GC, NI])
                    gp.tensor_tensor(vals[par][:, :, k, :], hot, col, ALU.mult).then_inc(p_val, 1)

            run(gp, NG, [(0, values)])
            gp.wait_ge(r_fit, 1)
            gp.wait_ge(a_rv, NG)
            gp.memset(hm0[:], 1.0).then_inc(s_id, 1)
            gp.memset(vv[:], 1.0).then_inc(s_id, 1)
            gp.wait_ge(s_id, 2)
            gp.affine_select(out=hm0[:].rearrange("p (a b) -> p a b", b=DH), in_=hm0[:].rearrange("p (a b) -> p a b", b=DH),
                             compare_op=ALU.is_ge, fill=0.0, base=0,
                             pattern=[[-DH, 128 // DH], [0, DH]], channel_multiplier=1).then_inc(s_id, 1)
            gp.wait_ge(s_id, 3)
            gp.affine_select(out=hmask[:].rearrange("p (a b) -> p a b", b=DH), in_=hm0[:].rearrange("p (a b) -> p a b", b=DH),
                             compare_op=ALU.is_ge, fill=0.0, base=DH - 1,
                             pattern=[[DH, 128 // DH], [0, DH]], channel_multiplier=-1).then_inc(s_id, 1)

            def add_bias(s, par):
                gp.wait_ge(v_ag, s + 1)
                gp.sem_inc(alone_gp, 1)
                gp.tensor_scalar(ve[:, par:par + 1], mv[:, par, 1:2], EPS, None, ALU.add).then_inc(p_ve, 1)
                gp.wait_ge(p_ve, s + 1)
                gp.tensor_tensor(rs[:, par:par + 1], ve[:, par:par + 1], mhalf[0:NB], ALU.pow).then_inc(v_rs, 1)
                gp.wait_ge(v_xn, s + 1)
                gp.tensor_tensor(x_sb[:, s, :], x_sb[:, s, :], bias[0:NB], ALU.add).then_inc(p_b, 1)

            gp.wait_ge(v_bias, 2)
            run(gp, NS, [(0, add_bias)])
            gp.wait_ge(y_out, 160)
            gp.wait_ge(v_at, G)
            fast = gp.value_load(fits[0:1, 0:1], min_val=0, max_val=1)
            with gp.If(fast == 1):
                gp.memset(y_hi[:, :, D:D + 2].bitcast(F32), 1.0).then_inc(p_one, 1)
                with gp.Fori(0, NG // 4) as j:
                    for k in range(4):
                        gp.wait_ge(w_in[k], j * 16)
                    gp.tensor_copy(wix[:, 0, :], window_ix[:, bass.ds(j * 4, 4)]).then_inc(w_ix, 1)
                    gp.wait_ge(w_ix, j + 1)
                    for k in range(4):
                        gp.wait_ge(v_lo, j * 4)
                        gp.sem_inc(alone_gp, 1)
                        gp.indirect_dma_start(raw[:, k, :], None, y_table,
                                              bass.IndirectOffsetOnAxis(ap=wix[:, 0, k:k + 1], axis=0)).then_inc(w_in[k], 16)
            with gp.If(fast == 0):
                gp.memset(src2[:], -1).then_inc(s_c, 1)
                gp.memset(dst2[:], 0).then_inc(s_c, 1)
                gp.memset(grow[:], 1.0).then_inc(s_c, 1)
                gp.iota(nodes[:], [[1, PASS], [NS, NB]], base=0, channel_multiplier=0,
                        allow_small_or_imprecise_dtypes=True).then_inc(s_c, 1)
                gp.wait_ge(s_c, 4)
                load_edges(gp, src2, dst2, s_e)
                gp.wait_ge(s_e, 96)

                def gather(it, j, first):
                    for hf in range(2):
                        if not first:
                            for k in range(UN // 2):
                                gp.wait_ge(g_in[hf * UN // 2 + k], it * 16)
                        gp.tensor_copy(ixb[:, hf, :], dst2[:, bass.ds(j * UN + hf * (UN // 2), UN // 2)]).then_inc(p_ix, 1)
                        gp.wait_ge(p_ix, it * 2 + hf + 1)
                        for k in range(UN // 2):
                            kk = hf * (UN // 2) + k
                            if not first:
                                gp.wait_ge(pe_e, it * UN - (UN - kk - 1))
                            gp.sem_inc(alone_gp, 1)
                            gp.indirect_dma_start(grow[:, kk, 0:D], None, y_table,
                                                  bass.IndirectOffsetOnAxis(ap=ixb[:, hf, k:k + 1], axis=0)
                                                  ).then_inc(g_in[kk], 16)

                STEPS = EC // UN
                gather(0, 0, True)
                with gp.Fori(1, STEPS) as j:
                    gather(j, j, False)
                with gp.Fori(1, NS // PASS) as r:
                    with gp.Fori(0, STEPS) as j:
                        gather(r * STEPS + j, j, False)
            gp.wait_ge(x1_ready, 1)
            gp.memset(off0[:], 0.0).then_inc(p_k, 1)
            gp.iota(iota_e[:], [[1, NE]], base=0, channel_multiplier=0, allow_small_or_imprecise_dtypes=True).then_inc(p_k, 1)
            gp.wait_ge(p_k, 2)
            gp.affine_select(out=off0[:].rearrange("p (a b) -> p a b", b=H), in_=off0[:].rearrange("p (a b) -> p a b", b=H),
                             compare_op=ALU.is_equal, fill=-BIG, base=0,
                             pattern=[[-1, NE], [0, H]], channel_multiplier=1).then_inc(p_k, 1)
            with gp.Fori(0, G) as g:
                for t in range(2):
                    gp.wait_ge(f_ag, g * 2 + t + 1)
                    gp.sem_inc(alone_gp, 1)
                    gp.tensor_scalar(fve[:, t:t + 1], fmv[:, t, 1:2], EPS, None, ALU.add).then_inc(p_ve, 1)
                    gp.wait_ge(p_ve, g * 2 + t + 1 + NS)
                    gp.tensor_tensor(frs[:, t:t + 1], fve[:, t:t + 1], mhalf[0:NB], ALU.pow).then_inc(f_rs, 1)

        @block.scalar
        def _(act):
            def store_slots(g, par):
                act.wait_ge(pe_rt, g + 1)
                act.copy(routed[:, :, :, bass.ds(g, 1)].rearrange("p k i a -> p k (i a)"),
                         ps[:, 2 + par, 0:2 * NI].rearrange("p (k i) -> p k i", k=2)).then_inc(a_rv, 1)

            run(act, NG, [(0, store_slots)])
            act.wait_ge(r_fit, 1)
            act.wait_ge(s_id, 4)

            def xt_copy(s, par):
                act.wait_ge(pe_tr, s + 1)
                wait(act, pe_yz, s - 1)
                act.copy(xt[:, par], ps[:, par, 0:250].rearrange("p (c n) -> p c n", c=2)).then_inc(a_xt, 1)
                act.copy(xnT[:, :, bass.ds(s * NB, NB)], ps[:, par, 0:250].rearrange("p (c n) -> p c n", c=2)).then_inc(a_xt2, 1)

            def kv_act(s, par):
                act.wait_ge(pe_kv, s + 1)
                wait(act, pe_cx, s - 1)
                act.copy(vv[:, par].rearrange("p (c n) -> p c n", c=2)[:, :, 0:128],
                         ps[0:NB, 2 + par, 256:512].rearrange("p (c n) -> p c n", c=2)).then_inc(a_v, 1)
                act.wait_ge(pe_yz, s + 1)
                act.copy(agg_sb[:, s, 0:D], ps[0:NB, 4 + par, 0:D]).then_inc(a_y, 1)
                act.wait_ge(v_km, s + 1)
                wait(act, v_kf, s - 1)
                act.activation(kx[:, par], km[:, par], ACT.Exp).then_inc(a_kx, 1)

            run(act, NS, [(0, xt_copy), (1, kv_act)])

            def q_exp(g, par):
                act.wait_ge(v_qm, g + 1)
                wait(act, v_qf, g - 1)
                act.activation(qx[par], qm[par], ACT.Exp).then_inc(a_qx, 1)

            run(act, G, [(0, q_exp)])

            def high(q):
                for t in range(2):
                    k = (2 * q + t) % 4 if isinstance(q, int) else t
                    act.wait_ge(w_in[k], 16 * ((2 * q + t) // 4 + 1))
                    act.copy(y_hi[:, 2 * q + t, 0:D], raw[:, k, :]).then_inc(a_hi, 1)

            def counts(n, par):
                act.wait_ge(pe_a, n + 1)
                wait(act, pe_d, n - 1)
                act.copy(cnt_T[par][:].rearrange("p t h n -> p (t h n)"), ps[:, par, :]).then_inc(a_cn, 1)

            act.wait_ge(v_at, G)
            fast = act.value_load(fits[0:1, 0:1], min_val=0, max_val=1)
            with act.If(fast == 1):
                for q in range(QP):
                    high(q)
                    if q >= 2:
                        counts(q - 2, q % 2)
                for q in range(QP - 2, QP):
                    counts(q, q % 2)
                with act.Fori(QP // 4, NI * QP // 4) as m:
                    for u in range(4):
                        counts(m * 4 + u, u % 2)
            act.wait_ge(s_f, 112)

            def xf_copy(g, par):
                act.wait_ge(f_tr, g + 1)
                act.wait_ge(f_h, g * JH)
                act.wait_ge(f_lg, g * 2)
                act.copy(xfT[:].rearrange("p c t n -> p (c t n)"), ps[:, 0, 0:500]).then_inc(f_xt, 1)
                act.wait_ge(f_ot, g + 1)
                act.copy(oeT[:].rearrange("p t n -> p (t n)"), ps[0:NE, 1, 0:250]).then_inc(f_os, 1)
                act.wait_ge(f_o, g * 2)
                for j in range(JH):
                    act.wait_ge(f_h, g * JH + j + 1)
                    act.activation(hs[:, j, :], ps[:, 2 + j % 2, 0:250], ACT.Relu, bias=b1_sb[:, j:j + 1]).then_inc(f_hs, 1)

            with act.Fori(0, G) as g:
                xf_copy(g, 0)

        @block.tensor
        def _(pe):
            pe.wait_ge(q_c, 14)
            pe.wait_ge(r_v, 1)
            pe.matmul(ps[:, 4, 0:NG], ones_f[0:1, :], df[0:1, :].rearrange("p (g c) -> p g c", c=GC)[:, :, 0:1].rearrange("p g a -> p (g a)"),
                      start=True, stop=True).then_inc(pe_base, 1)

            def ranks(g, par):
                pe.wait_ge(r_pre, g + 1)
                wait(pe, r_prod, g - 1)
                total = pre[par][:].rearrange("p (i c) -> p i c", c=GC)[:, :, GC - 1:GC].to_broadcast([128, NI, GC])
                pe.matmul(ps[:, par, 0:NW], before[:], total, start=True, stop=False)
                pe.matmul(ps[:, par, 0:NW], ident_b[:], pre[par][:], start=False, stop=True).then_inc(pe_rk, 1)

            def route(g, par):
                pe.wait_ge(r_ohr, g + 1)
                pe.wait_ge(p_val, g * 2 + 2)
                wait(pe, a_rv, g - 1)
                for c in range(GC):
                    mm = pe.matmul(ps[:, 2 + par, 0:2 * NI], ohr[par][:, c, :], vals[par][:, c].rearrange("p k i -> p (k i)"),
                                   start=(c == 0), stop=(c == GC - 1))
                mm.then_inc(pe_rt, 1)

            run(pe, NG, [(0, ranks), (1, route)])
            pe.wait_ge(r_ready, 1)
            pe.matmul(ps[0:1, 5, 0:1], good[:, 3:4], ones_f[:, 0:1], start=True, stop=True).then_inc(pe_fit, 1)
            pe.wait_ge(r_fit, 1)
            pe.wait_ge(a_rv, NG)
            pe.wait_ge(s_id, 4)
            pe.wait_ge(s_w, 80)

            def tr(s, par):
                pe.wait_ge(v_xn, s + 1)
                wait(pe, a_xt2, s - 1)
                for c in range(2):
                    mm = pe.transpose(ps[:, par, c * NB:(c + 1) * NB], xn[:, par, c * 128:(c + 1) * 128], ident[0:NB, 0:NB])
                mm.then_inc(pe_tr, 1)

            def kvyz(s, par):
                pe.wait_ge(a_xt, s + 1)
                wait(pe, v_kf, s - 1)
                wait(pe, a_v, s - 1)
                for c in range(2):
                    mm = pe.matmul(ps[0:NB, 2 + par, :], xt[:, par, c, :], wkv_sb[:, c, :], start=(c == 0), stop=(c == 1))
                mm.then_inc(pe_kv, 1)
                wait(pe, a_y, s - 1)
                wait(pe, v_base, s - 1)
                for c in range(2):
                    mm = pe.matmul(ps[0:NB, 4 + par, :], xt[:, par, c, :], wyz_sb[:, c, :], start=(c == 0), stop=(c == 1))
                mm.then_inc(pe_yz, 1)

            def context(s, par):
                pe.wait_ge(v_kf, s + 1)
                pe.wait_ge(a_v, s + 1)
                for c in range(2):
                    mm = pe.matmul(ps[:, 6 + c, 0:129], kf[:, par, c * 128:(c + 1) * 128], vv[:, par, c * 129:(c + 1) * 129],
                                   start=False, stop=False, skip_group_check=True) if not (isinstance(s, int) and s in (0, NS - 1)) else \
                        pe.matmul(ps[:, 6 + c, 0:129], kf[:, par, c * 128:(c + 1) * 128], vv[:, par, c * 129:(c + 1) * 129],
                                  start=(s == 0), stop=(s == NS - 1), skip_group_check=True)
                mm.then_inc(pe_cx, 1)

            run(pe, NS, [(0, tr), (1, kvyz), (2, context)])
            pe.wait_ge(v_bd, 4)
            for c in range(2):
                mm = pe.transpose(ps[:, 0, c * 128:(c + 1) * 128], cbd[:, c, :], ident[:])
            mm.then_inc(pe_ct, 1)
            pe.wait_ge(v_ct, 1)
            for c in range(2):
                mm = pe.matmul(ps[:, 1, c * 256:(c + 1) * 256], cbdT[:, c, :], wp_sb[:, c, :], start=True, stop=True)
            mm.then_inc(pe_m, 1)

            def q(g, par):
                wait(pe, v_qf, g - 1)
                if isinstance(g, int) and g < 2:
                    pe.wait_ge(v_m, 1)
                    pe.wait_ge(a_xt2, NS)
                for o in range(2):
                    for c in range(2):
                        mm = pe.matmul(ps[:, 2 + par, o * 250:(o + 1) * 250], wq_sb[:, c, o * 128:(o + 1) * 128],
                                       xnT[:, c, bass.ds(g * 250, 250)], start=(c == 0), stop=(c == 1))
                mm.then_inc(pe_q, 1)

            def den(g, par):
                pe.wait_ge(v_qf, g + 1)
                wait(pe, v_dn, g - 1)
                for o in range(2):
                    mm = pe.matmul(ps[:, 4 + par, o * 250:(o + 1) * 250], ksb[:, o, :], qf[par][:, o * 250:(o + 1) * 250],
                                   start=True, stop=True)
                mm.then_inc(pe_dn, 1)

            def att(g, par):
                pe.wait_ge(v_qs, g + 1)
                wait(pe, v_at, g - 1)
                for t in range(2):
                    for o in range(2):
                        mm = pe.matmul(ps[0:NB, 6 + par, t * 256:(t + 1) * 256],
                                       qs[par][:, o * 250 + t * NB:o * 250 + (t + 1) * NB], msb[:, o, :],
                                       start=(o == 0), stop=(o == 1))
                mm.then_inc(pe_at, 1)

            run(pe, G, [(0, q), (1, den), (2, att)])
            pe.wait_ge(v_at, G)

            def count(n, buf, par):
                pe.wait_ge(v_o, n + 1)
                wait(pe, a_cn, n - 1)
                for t in range(2):
                    mm = pe.matmul(ps[:, par, t * 256:(t + 1) * 256], oht[:, buf, t, :], ohs[:, buf, t, :], start=True, stop=True)
                mm.then_inc(pe_a, 1)

            def add_up(n, q, par, first, last):
                pe.wait_ge(a_cn, n + 1)
                for t in range(2):
                    g = q * 2 + t
                    for h in range(2):
                        w = cnt_T[par][:, t, h, 0:NB + 1]
                        pe.matmul(ps[0:NB + 1, 2 + h, 0:D + 2], w, y_hi[:, g, :], start=(first and t == 0), stop=False)
                        mm = pe.matmul(ps[0:NB + 1, 2 + h, 0:D], w, y_lo[:, g, :], start=False, stop=(last and t == 1))
                mm.then_inc(pe_d, 1)

            def block_sums(i, n0, windows):
                def ready(q):
                    if windows:
                        pe.wait_ge(v_lo, q * 2 + 2)
                        if q == 0:
                            pe.wait_ge(p_one, 1)
                for q in range(4):
                    count(n0 + q, q, q % 2)
                    if q:
                        if q == 1 and not windows:
                            pe.wait_ge(v_ev, i)
                        ready(q - 1)
                        add_up(n0 + (q - 1), q - 1, (q - 1) % 2, q == 1, False)
                with pe.Fori(1, QP // 4) as m:
                    for u in range(4):
                        count(n0 + m * 4 + u, u, u % 2)
                        if windows:
                            pe.wait_ge(v_lo, m * 8 + u * 2)
                        add_up(n0 + m * 4 + (u - 1), m * 4 + (u - 1), (u - 1) % 2, False, False)
                ready(QP - 1)
                add_up(n0 + (QP - 1), QP - 1, (QP - 1) % 2, False, True)

            fast = pe.value_load(fits[0:1, 0:1], min_val=0, max_val=1)
            with pe.If(fast == 1):
                block_sums(0, 0, True)
                with pe.Fori(1, NI) as i:
                    block_sums(i, i * QP, False)

            def edges(it, first, last):
                for k in range(UN):
                    pe.wait_ge(g_in[k], it * 16 + 16)
                    pe.wait_ge(v_oh, it * UN + k + 1)
                    for c in range(PASS):
                        mm = pe.matmul(ps[0:NB, c, 0:D + 1], oneh[:, k % 2, c * NB:(c + 1) * NB], grow[:, k, :],
                                       start=(first and k == 0), stop=(last and k == UN - 1), skip_group_check=True)
                    mm.then_inc(pe_e, 1)

            STEPS = EC // UN
            with pe.If(fast == 0):
                pe.wait_ge(s_c, 4)
                with pe.Fori(0, NS // PASS) as r:
                    pe.wait_ge(v_agg, r)
                    edges(r * STEPS, True, False)
                    with pe.Fori(1, STEPS - 1) as j:
                        edges(r * STEPS + j, False, False)
                    edges(r * STEPS + (STEPS - 1), False, True)

            pe.wait_ge(x1_ready, 1)
            pe.wait_ge(p_k, 3)
            pe.wait_ge(s_f, 112)

            def ffn(g):
                pe.wait_ge(f_xf, g * 2 + 2)
                for c in range(2):
                    for t in range(2):
                        mm = pe.transpose(ps[:, 0, c * 250 + t * NB:c * 250 + (t + 1) * NB], fxf[:, t, c * 128:(c + 1) * 128],
                                          ident[0:NB, 0:NB])
                mm.then_inc(f_tr, 1)
                pe.wait_ge(f_xt, g + 1)
                for t in range(2):
                    for c in range(2):
                        mm = pe.matmul(ps[0:NB, 1, t * NE:(t + 1) * NE], xfT[:, c, t, :], rw_sb[:, c, :], start=(c == 0), stop=(c == 1))
                    mm.then_inc(f_lg, 1)
                pe.wait_ge(f_oh, g * 2 + 2)
                for t in range(2):
                    mm = pe.transpose(ps[0:NE, 1, t * NB:(t + 1) * NB], oe[:, t, :], ident[0:NB, 0:NB])
                mm.then_inc(f_ot, 1)
                pe.wait_ge(f_os, g + 1)
                for j in range(JH):
                    wait(pe, f_hs, g * JH + j - 1) if j else None
                    for c in range(2):
                        pe.matmul(ps[:, 2 + j % 2, 0:250], w1_sb[:, c, j * 128:(j + 1) * 128],
                                  xfT[:, c].rearrange("p t n -> p (t n)"), start=(c == 0), stop=False)
                    pe.matmul(ps[:, 2 + j % 2, 0:250], off0[:, j * 128:(j + 1) * 128], oeT[:].rearrange("p t n -> p (t n)"),
                              start=False, stop=True).then_inc(f_h, 1)
                pe.wait_ge(f_hs, g * JH + JH)
                pe.wait_ge(f_r, g * 2)
                for t in range(2):
                    for j in range(JH):
                        pe.matmul(ps[0:NB, 4 + t, 0:D], hs[:, j, t * NB:(t + 1) * NB], w2_sb[:, j, :], start=(j == 0), stop=False)
                    pe.matmul(ps[0:NB, 4 + t, 0:D], oeT[:, t, :], b2_sb[:], start=False, stop=True).then_inc(f_o, 1)

            with pe.Fori(0, G) as g:
                ffn(g)

        @block.vector
        def _(v):
            steps = [0]

            def then(ins):
                steps[0] += 1
                ins.then_inc(r_v, 1)
                v.wait_ge(r_v, steps[0])

            v.wait_ge(r_ld, 96)
            then(v.tensor_copy(df[:], dst_i[:]))
            then(v.tensor_copy(sf[:], src_i[:]))
            then(v.tensor_scalar(tf[:], sf[:], -(NS - 1) / 2, 1.0 / NS, ALU.add, ALU.mult))
            then(v.tensor_copy(bi[:], tf[:]))
            then(v.tensor_copy(bf[:], bi[:]))
            then(v.scalar_tensor_tensor(tile_f[:], bf[:], -float(NS), sf[:], ALU.mult, ALU.add))
            then(v.tensor_scalar(tf[:], tile_f[:], 0.5, -0.25, ALU.mult, ALU.add))
            then(v.tensor_copy(bi[:], tf[:]))
            then(v.tensor_copy(blk[:], bi[:]))
            then(v.scalar_tensor_tensor(tf[:], blk[:], -2.0, tile_f[:], ALU.mult, ALU.add))
            then(v.scalar_tensor_tensor(tf[:], tf[:], 128.0, bf[:], ALU.mult, ALU.add))
            then(v.tensor_scalar(vs[:], tf[:], 1.0, None, ALU.add))
            then(v.tensor_scalar(valid[:], sf[:], 0.0, None, ALU.is_ge))
            then(v.tensor_scalar(tf[:], valid[:], -1000.0, 1000.0, ALU.mult, ALU.add))
            then(v.tensor_tensor(blk[:], blk[:], tf[:], ALU.add))
            v.wait_ge(pe_base, 1)
            then(v.tensor_copy(base_f[:], ps[:, 4, 0:NG]))
            then(v.tensor_tensor(tf[:].rearrange("p (g c) -> p g c", c=GC), df[:].rearrange("p (g c) -> p g c", c=GC),
                                 base_f[:].rearrange("p (g a) -> p g a", a=1).to_broadcast([128, NG, GC]), ALU.subtract))
            then(v.tensor_scalar(vd[:], tf[:], 1.0, None, ALU.add))
            then(v.tensor_tensor(tf[:], tf[:], valid[:], ALU.mult))
            then(v.tensor_reduce(top[:, 0:1], tf[:], mybir.AxisListType.X, ALU.max))
            then(v.tensor_reduce(top[:, 1:2], tf[:], mybir.AxisListType.X, ALU.min))
            then(v.tensor_scalar(win_f[:], base_f[:], pcol[:, 0:1], float(N - 1), ALU.add, ALU.min))
            then(v.tensor_copy(window_ix[:], win_f[:]))
            v.wait_ge(q_c, 14)

            def hot_block(g, par):
                wait(v, p_val, 2 * (g - 1))
                col = blk[:, bass.ds(g * GC, GC)].rearrange("p (a c) -> p a c", a=1).to_broadcast([128, NI, GC])
                v.tensor_tensor(ohI[par][:].rearrange("p (i c) -> p i c", c=GC), col,
                                iota_i[:].rearrange("p (i a) -> p i a", a=1).to_broadcast([128, NI, GC]), ALU.is_equal).then_inc(r_oh, 1)
                v.wait_ge(r_oh, g + 1)
                wait(v, pe_rk, g - 1)
                v.sem_inc(alone_v, 1)
                v.tensor_tensor_scan(pre[par][:], restart[:], ohI[par][:], 0.0, ALU.mult, ALU.add).then_inc(r_pre, 1)

            def hot_rank(g, par):
                v.wait_ge(pe_rk, g + 1)
                v.scalar_tensor_tensor(prod[par][:], ps[:, par, 0:NW], -1.0, ohI[par][:], ALU.add, ALU.mult).then_inc(r_prod, 1)
                v.wait_ge(r_prod, g + 1)
                wait(v, pe_rt, g - 1)
                v.tensor_reduce(rank[:, bass.ds(g * GC, GC)], prod[par][:].rearrange("p (i c) -> p c i", c=GC),
                                mybir.AxisListType.X, ALU.add).then_inc(r_r, 1)
                v.wait_ge(r_r, g + 1)
                for c in range(GC):
                    last = v.tensor_scalar(ohr[par][:, c, :], iota_r[:], rank[:, bass.ds(g * GC + c, 1)], None, ALU.is_equal)
                last.then_inc(r_ohr, 1)

            run(v, NG, [(0, hot_block), (1, hot_rank)])
            v.wait_ge(r_r, NG)
            then(v.tensor_reduce(top[:, 2:3], rank[:], mybir.AxisListType.X, ALU.max))
            then(v.tensor_scalar(good[:, 0:1], top[:, 0:1], 127.0, None, ALU.is_le))
            then(v.tensor_scalar(good[:, 1:2], top[:, 1:2], 0.0, None, ALU.is_ge))
            then(v.tensor_scalar(good[:, 2:3], top[:, 2:3], 127.0, None, ALU.is_le))
            then(v.tensor_tensor(good[:, 0:1], good[:, 0:1], good[:, 1:2], ALU.mult))
            v.tensor_tensor(good[:, 3:4], good[:, 0:1], good[:, 2:3], ALU.mult).then_inc(r_ready, 1)
            v.wait_ge(pe_fit, 1)
            v.tensor_scalar(fits[:], ps[0:1, 5, 0:1], 128.0, None, ALU.is_equal).then_inc(r_fit, 1)
            v.wait_ge(r_fit, 1)
            v.wait_ge(a_rv, NG)
            v.wait_ge(s_w, 80)
            v.tensor_tensor(biast[:], bias_sb[:, 0], bias_sb[:, 1], ALU.add).then_inc(v_bias, 1)
            v.wait_ge(v_bias, 1)
            v.tensor_tensor(bias[:], biast[:], bias_sb[:, 2], ALU.add).then_inc(v_bias, 1)
            v.wait_ge(s_in, 32)

            def norm(s, par):
                wait(v, v_rs, s - 1)
                v.sem_inc(alone_v, 1)
                v.bn_stats(st[:, par], x_sb[:, s, :]).then_inc(v_st, 1)
                v.wait_ge(v_st, s + 1)
                v.sem_inc(alone_v, 1)
                v.bn_aggr(mv[:, par], st[:, par]).then_inc(v_ag, 1)
                v.wait_ge(v_ag, s + 1)
                v.wait_ge(v_rs, s + 1)
                wait(v, pe_tr, s - 1)
                v.tensor_scalar(xn[:, par], x_sb[:, s, :], mv[:, par, 0:1], rs[:, par:par + 1], ALU.subtract, ALU.mult).then_inc(v_xn, 1)

            def kv_dve(s, par):
                v.wait_ge(a_v, s + 1)
                wait(v, a_kx, s - 1)
                v.tensor_scalar(km[:, par], ps[0:NB, 2 + par, 0:256], 0.0, None, ALU.min).then_inc(v_km, 1)
                v.wait_ge(a_y, s + 1)
                v.wait_ge(p_b, s + 1)
                v.tensor_tensor(x_sb[:, s, :], x_sb[:, s, :], ps[0:NB, 4 + par, 256:512], ALU.add).then_inc(v_base, 1)
                v.wait_ge(a_kx, s + 1)
                wait(v, pe_cx, s - 1)
                v.scalar_tensor_tensor(kf[:, par], ps[0:NB, 2 + par, 0:256], 0.0, kx[:, par], ALU.max, ALU.add).then_inc(v_kf, 1)

            run(v, NS, [(0, norm), (1, kv_dve)])
            v.wait_ge(pe_cx, NS)
            v.wait_ge(s_id, 4)
            for c in range(2):
                v.tensor_copy(cx[:, c], ps[:, 6 + c, 0:129]).then_inc(v_cx, 1)
            v.wait_ge(v_cx, 2)
            for c in range(2):
                v.tensor_tensor(cbd[:, c], cx[:, c, 0:128], hmask[:], ALU.mult).then_inc(v_bd, 1)
                v.tensor_scalar(ksb[:, c], hmask[:], cx[:, c, 128:129], None, ALU.mult).then_inc(v_bd, 1)
            v.wait_ge(pe_ct, 1)
            v.tensor_copy(cbdT[:].rearrange("p c n -> p (c n)"), ps[:, 0, 0:256]).then_inc(v_ct, 1)
            v.wait_ge(pe_m, 1)
            v.tensor_copy(msb[:].rearrange("p c n -> p (c n)"), ps[:, 1, :]).then_inc(v_m, 1)

            def q_min(g, par):
                v.wait_ge(pe_q, g + 1)
                wait(v, a_qx, g - 1)
                v.tensor_scalar(qm[par], ps[:, 2 + par, 0:500], 0.0, None, ALU.min).then_inc(v_qm, 1)
                v.wait_ge(a_qx, g + 1)
                wait(v, pe_dn, g - 1)
                v.scalar_tensor_tensor(qf[par], ps[:, 2 + par, 0:500], 0.0, qx[par], ALU.max, ALU.add).then_inc(v_qf, 1)

            def q_scale(g, par):
                v.wait_ge(pe_dn, g + 1)
                v.tensor_scalar(dn[par], ps[:, 4 + par, 0:500], 1e-6, None, ALU.max).then_inc(v_dn, 1)
                v.wait_ge(v_dn, g + 1)
                v.reciprocal(qm2[par], dn[par]).then_inc(v_rc, 1)
                v.wait_ge(v_rc, g + 1)
                wait(v, pe_at, g - 1)
                v.tensor_tensor(qs[par], qf[par], qm2[par], ALU.mult).then_inc(v_qs, 1)

            def base(g, par):
                v.wait_ge(pe_at, g + 1)
                v.tensor_tensor(x_sb[:, bass.ds(g * 2, 2), :], x_sb[:, bass.ds(g * 2, 2), :],
                                ps[0:NB, 6 + par, :].rearrange("p (t d) -> p t d", t=2), ALU.add).then_inc(v_at, 1)

            run(v, G, [(0, q_min), (1, q_scale), (2, base)])
            v.wait_ge(v_at, G)

            def low(q):
                for t in range(2):
                    v.wait_ge(a_hi, 2 * q + t + 1)
                    v.tensor_tensor(y_lo[:, 2 * q + t, :], raw[:, (2 * q + t) % 4, :], y_hi[:, 2 * q + t, 0:D].bitcast(F32),
                                    ALU.subtract).then_inc(v_lo, 1)

            def hot_slots(n, q, buf, i):
                wait(v, pe_a, n - (RING - 1))
                for t in range(2):
                    c = i * NG + q * 2 + t
                    v.tensor_scalar(oht[:, buf, t, :], iota_b[:, 0:128], routed[:, 0].rearrange("p i g -> p (i g)")[:, bass.ds(c, 1)],
                                    None, ALU.is_equal)
                    last = v.tensor_scalar(ohs[:, buf, t, :], iota_b[:], routed[:, 1].rearrange("p i g -> p (i g)")[:, bass.ds(c, 1)],
                                           None, ALU.is_equal)
                last.then_inc(v_o, 1)

            def means(i):
                v.wait_ge(pe_d, i * QP + QP)
                v.tensor_scalar(cm[:], ps[0:NB, 2:4, D], 1.0, None, ALU.max).then_inc(v_cm, 1)
                v.wait_ge(v_cm, i + 1)
                v.reciprocal(cr[:], cm[:]).then_inc(v_cr, 1)
                v.wait_ge(v_cr, i + 1)
                for h in range(2):
                    last = v.scalar_tensor_tensor(x_sb[:, i * 2 + h, :], ps[0:NB, 2 + h, 0:D], cr[:, h:h + 1], x_sb[:, i * 2 + h, :],
                                                  ALU.mult, ALU.add)
                last.then_inc(v_ev, 1)

            fast = v.value_load(fits[0:1, 0:1], min_val=0, max_val=1)
            with v.If(fast == 1):
                for q in range(QP):
                    hot_slots(q, q, q % RING, 0)
                    low(q)
                with v.Fori(1, NI) as i:
                    for q in range(RING):
                        hot_slots(i * QP + q, q, q, i)
                    means(i - 1)
                    with v.Fori(1, QP // RING) as m:
                        for u in range(RING):
                            hot_slots(i * QP + m * RING + u, m * RING + u, u, i)
                means(NI - 1)
                v.wait_ge(v_ev, NI)
            with v.If(fast == 0):
                v.wait_ge(s_c, 4)
                v.wait_ge(s_e, 96)
                v.tensor_copy(srcf[:], src2[:]).then_inc(v_sub, 1)
                STEPS = EC // UN

                def hot(it, j):
                    for k in range(UN):
                        v.wait_ge(pe_e, it * UN + k - 1)
                        v.tensor_scalar(oneh[:, k % 2], nodes[:].rearrange("p a b -> p (a b)"),
                                        srcf[:, bass.ds(j * UN + k, 1)], None, ALU.is_equal).then_inc(v_oh, 1)

                with v.Fori(0, NS // PASS) as r:
                    v.wait_ge(v_sub, r + 1)
                    for k in range(UN):
                        v.wait_ge(pe_e, r * STEPS * UN + (k - 1 if k >= 2 else 0))
                        v.tensor_scalar(oneh[:, k % 2], nodes[:].rearrange("p a b -> p (a b)"), srcf[:, k:k + 1], None, ALU.is_equal).then_inc(v_oh, 1)
                    with v.Fori(1, STEPS) as j:
                        hot(r * STEPS + j, j)
                    v.wait_ge(pe_e, r * STEPS * UN + STEPS * UN)
                    v.tensor_copy(agg2[:, bass.ds(r * PASS, PASS), :], ps[0:NB, 0:PASS, 0:D + 1]).then_inc(v_agg, 1)
                    v.wait_ge(v_oh, r * STEPS * UN + STEPS * UN)
                    v.tensor_scalar(srcf[:], srcf[:], -float(PASS), None, ALU.add).then_inc(v_sub, 1)

                v.wait_ge(v_agg, NS // PASS)
                v.tensor_scalar(rc0[:], agg2[:, :, D], 1.0, None, ALU.max).then_inc(b_rc, 1)
                v.wait_ge(b_rc, 1)
                v.reciprocal(rc[:], rc0[:]).then_inc(b_rc, 1)
                v.wait_ge(b_rc, 2)
                with v.Fori(0, NS) as t:
                    v.scalar_tensor_tensor(x_sb[:, t, :], agg2[:, t, 0:D], rc[:, bass.ds(t, 1)], x_sb[:, t, :], ALU.mult, ALU.add).then_inc(b_x1, 1)
                v.wait_ge(b_x1, NS)
            v.sem_inc(x1_ready, 1)
            v.wait_ge(s_f, 112)
            v.wait_ge(p_k, 3)

            with v.Fori(0, G) as g:
                for t in range(2):
                    s = g * 2 + t
                    v.bn_stats(fst[:, t], x_sb[:, s, :]).then_inc(f_st, 1)
                    v.wait_ge(f_st, s + 1)
                    v.sem_inc(alone_v, 1)
                    v.bn_aggr(fmv[:, t], fst[:, t]).then_inc(f_ag, 1)
                    v.wait_ge(f_ag, s + 1)
                    v.wait_ge(f_rs, s + 1)
                    v.wait_ge(f_tr, g)
                    v.tensor_scalar(fxf[:, t], x_sb[:, s, :], fmv[:, t, 0:1], frs[:, t:t + 1], ALU.subtract, ALU.mult).then_inc(f_xf, 1)
                for t in range(2):
                    s = g * 2 + t
                    v.wait_ge(f_lg, g * 2 + 2)
                    v.tensor_tensor(lg[:, t], ps[0:NB, 1, t * NE:(t + 1) * NE], rb_sb[0:NB], ALU.add).then_inc(f_lb, 1)
                    v.wait_ge(f_lb, s + 1)
                    v.sem_inc(alone_v, 1)
                    v.max(mx[:, t], lg[:, t]).then_inc(f_mx, 1)
                    v.wait_ge(f_mx, s + 1)
                    v.sem_inc(alone_v, 1)
                    v.max_index(mi[:, t], mx[:, t], lg[:, t]).then_inc(f_ix, 1)
                    v.wait_ge(f_ix, s + 1)
                    v.tensor_copy(mf[:, t], mi[:, t, 0:1]).then_inc(f_if, 1)
                    v.wait_ge(f_if, s + 1)
                    v.wait_ge(f_ot, g)
                    v.tensor_scalar(oe[:, t], iota_e[0:NB], mf[:, t], None, ALU.is_equal).then_inc(f_oh, 1)
                for t in range(2):
                    s = g * 2 + t
                    v.wait_ge(f_o, s + 1)
                    v.scalar_tensor_tensor(x_sb[:, s, :], ps[0:NB, 4 + t, 0:D], 0.0, x_sb[:, s, :], ALU.max, ALU.add).then_inc(f_y, 1)
                v.wait_ge(f_y, g * 2 + 2)
                v.nop().then_inc(f_r, 2)


_OUT = ((N, D), "float32")


def kernel(**inputs):
    import numpy as np
    import concourse.bacc as bacc
    from concourse.bass_utils import run_bass_kernel_spmd as launch

    a = {k: np.asarray(v) for k, v in inputs.items()}
    lay = {
        "x": a["x"], "src": a["src"], "dst": a["dst"],
        "wkv": a["L0_mix_Wkv"].T, "wyz": np.concatenate([a["L0_gnn_W2"].T, a["L0_gnn_W1"].T], 1),
        "wq": a["L0_mix_Wq"].T, "wproj": a["L0_mix_Wproj"].T,
        "bias3": np.stack([a["L0_gnn_b1"], a["L0_gnn_b2"], a["L0_mix_bproj"]]),
        "rw": a["L0_ffn_router_w"].T, "rb": a["L0_ffn_router_b"],
        "w1": a["L0_ffn_W1"], "b1": a["L0_ffn_b1"].reshape(JH, 128).T,
        "w2": a["L0_ffn_W2"].reshape(NE * H, D), "b2": a["L0_ffn_b2"],
    }
    nc = bacc.Bacc("TRN2", target_bir_lowering=False, num_devices=1)
    arrays, args = {}, []
    for name, v in lay.items():
        v = np.ascontiguousarray(v)
        arrays[f"in_{name}"] = v
        args.append(nc.dram_tensor(f"in_{name}", v.shape, mybir.dt.from_np(v.dtype), kind="ExternalInput").ap())
    args.append(nc.dram_tensor("out_0", _OUT[0], F32, kind="ExternalOutput").ap())
    gps_layer(nc, *args)
    r = launch(nc, [arrays], core_ids=[0])
    return r.results[0]["out_0"]
```

```python
from contextlib import ExitStack

import concourse.bass as bass
from concourse import mybir

ALU = mybir.AluOpType
ACT = mybir.ActivationFunctionType
F32 = mybir.dt.float32
I32 = mybir.dt.int32
U32 = mybir.dt.uint32

N, D = 6250, 256
NB, NS = 125, 50
E = 106250
GC = 15
NG = 56
GE = 128 * GC
EC = NG * GC
NI = NS // 2
NW = NI * GC
QP = NG // 2
RING = 4
DH = 32
NE, H = 32, 64
TT = 82
CH = TT // 2
RAW = 12
AHEAD = NG - NS
RG = 10
G = NS // 2
PASS = 5
UN = 8
EPS = 1e-5
BF16 = mybir.dt.bfloat16
F32R = mybir.dt.float32r


def wait(eng, sem, value):
    if isinstance(value, int) and value <= 0:
        return
    eng.wait_ge(sem, value)


def run(eng, n, stages, peel=4):
    run_mixed(eng, [(lag, n, work) for lag, work in stages], peel)


def run_mixed(eng, stages, peel):
    turns = (min(lag + n for lag, n, _ in stages) - peel) // 2

    def static(step):
        for lag, n, work in stages:
            if 0 <= step - lag < n:
                work(step - lag, (step - lag) % 2)

    for step in range(peel):
        static(step)
    with eng.Fori(0, turns) as i:
        for u in range(peel, peel + 2):
            for lag, n, work in stages:
                work(i * 2 + (u - lag), (u - lag) % 2)
    for step in range(peel + 2 * turns, max(lag + n for lag, n, _ in stages)):
        static(step)


def run4(eng, n, stages, peel=8):
    lag = max(l for l, _ in stages)
    turns = (n - peel) // 4

    def static(step):
        for l, work in stages:
            if 0 <= step - l < n:
                work(step - l, (step - l) % 4, (step - l) // 4)

    for step in range(peel):
        static(step)
    with eng.Fori(0, turns) as i:
        for u in range(peel, peel + 4):
            for l, work in stages:
                work(i * 4 + (u - l), (u - l) % 4, i + (u - l) // 4)
    for step in range(peel + 4 * turns, n + lag):
        static(step)


def gps_layer(nc, x, src, dst, wkv, wyz, wq, wproj, bias3, rw, rb, w1, b1, w2, b2, out):
    y_table = nc.dram_tensor("y_table", [N, D], F32).ap()
    tokens_in = nc.dram_tensor("tokens_in", [TT * 128, D], F32).ap()
    tokens_out = nc.dram_tensor("tokens_out", [TT * 128, D], F32).ap()
    with ExitStack() as ctx:
        def sb(name, shape, dt=F32):
            return ctx.enter_context(nc.sbuf_tensor(name, shape, dt))

        def sem(name):
            return ctx.enter_context(nc.semaphore(name))

        ps = ctx.enter_context(nc.psum_tensor("ps", [128, 8, 512], F32))

        x_sb = sb("x_sb", [NB, NS, D])
        routed = sb("routed", [128, 2, NI, NG])
        ident = sb("ident", [128, 128])
        mhalf = sb("mhalf", [128, 1])
        pcol = sb("pcol", [128, 1])
        iota_b = sb("iota_b", [128, 256], BF16)
        window_ix = sb("window_ix", [128, NG], U32)
        fits = sb("fits", [1, 1], I32)
        raw = sb("raw", [128, RAW, D])[:]
        wix = sb("wix", [128, RAW // 4, 4], U32)[:]

        phase = ExitStack()

        def pb(name, shape, dt=F32):
            return phase.enter_context(nc.sbuf_tensor(name, shape, dt))[:]

        prep = ExitStack()

        def prep_buffer(name, dt=F32):
            return prep.enter_context(nc.sbuf_tensor(name, [128, EC], dt))

        src_i, dst_i, bi = (prep_buffer(n, I32) for n in ("src_i", "dst_i", "bi"))
        sf, df, tf, bf, tile_f, valid = (prep_buffer(n) for n in ("sf", "df", "tf", "bf", "tile_f", "valid"))
        w_raw = prep.enter_context(nc.sbuf_tensor("w_raw", [128, 2, 2, 2 * D], F32))
        prep.close()
        xnT = pb("xnT", [128, 2, N])
        blk, vs, vd, rank = (pb(n, [128, EC], BF16) for n in ("blk", "vs", "vd", "rank"))
        zeros = pb("zeros", [128, D])
        base_f = pb("base_f", [128, NG])
        win_f = pb("win_f", [128, NG])
        iota_i = pb("iota_i", [128, NW], BF16)
        iota_r = pb("iota_r", [128, 128 * GC], BF16)
        restart = pb("restart", [128, NW], BF16)
        ident_b = pb("ident_b", [128, 128], BF16)
        before = pb("before", [128, 128], BF16)
        ones_f = pb("ones_f", [128, 128])
        ohI = [pb(f"ohI{k}", [128, NW], BF16) for k in range(2)]
        pre = [pb(f"pre{k}", [128, NW], BF16) for k in range(2)]
        prod = [pb(f"prod{k}", [128, NW]) for k in range(2)]
        vals = [pb(f"vals{k}", [128, 2, NI, GC], BF16) for k in range(2)]
        ohr = [pb(f"ohr{k}", [128, 128, GC], BF16) for k in range(2)]
        top = pb("top", [128, 4])
        good = pb("good", [128, 4])

        yz = pb("yz", [NB, 2, 2 * D])
        first = ExitStack()
        wkv_h, wkv_l, wyz_h, wyz_l = (first.enter_context(nc.sbuf_tensor(n, [128, 2, 2 * D], F32R))[:]
                                      for n in ("wkv_h", "wkv_l", "wyz_h", "wyz_l"))
        first.close()
        qx, dn, qf, qr = ([pb(f"{n}{k}", [128, 500]) for k in range(2)] for n in ("qx", "dn", "qf", "qr"))
        qs = dn
        pb("beyond_weights", [128, 96])
        wq_sb = pb("wq_sb", [128, 2, D])
        wp_sb = pb("wp_sb", [128, 2, D])
        bias_sb = pb("bias_sb", [128, 3, D])
        bias = pb("bias", [128, D])
        biast = bias_sb[:, 0]
        st = pb("st", [NB, 2, 6])
        mv = pb("mv", [NB, 2, 2])
        ve = pb("ve", [NB, 2])
        rs = pb("rs", [NB, 2])
        xn = pb("xn", [NB, 2, D])
        xt_h = pb("xt_h", [128, 2, 2, NB], F32R)
        xt_l = pb("xt_l", [128, 2, 2, NB], F32R)
        kx = pb("kx", [NB, 2, D])
        kf = pb("kf", [NB, 2, D])
        vv = pb("vv", [NB, 2, D + 2])
        cx = pb("cx", [128, 2, 129])
        cbd = pb("cbd", [128, 2, 128])
        cbdT = pb("cbdT", [128, 2, 128])
        hmask = pb("hmask", [128, 128])
        hm0 = pb("hm0", [128, 128])
        ksb = pb("ksb", [128, 2, 128])
        msb = pb("msb", [128, 2, D])
        at = [yz[:, k].rearrange("p (t d) -> p t d", t=2) for k in range(2)]
        phase.close()

        rw_sb = sb("rw_sb", [128, 2, NE])[:]
        fst = sb("fst", [NB, 2, 6])[:]
        fmv = sb("fmv", [NB, 2, 2])[:]
        mean = sb("mean", [NB, NS])[:]
        frs = sb("frs", [NB, NS])[:]
        fve = sb("fve", [NB, 2])[:]
        fxf = sb("fxf", [NB, 2, D])[:]
        xfT = sb("xfT", [128, 2, 250])[:]
        lg = sb("lg", [NB, NS, NE])[:]

        y_hi = pb("y_hi", [128, NG, D + 2], F32R)
        y_lo = pb("y_lo", [128, NG, D], F32R)
        cnt_T = [pb(f"cnt_T{k}", [128, 2, 2, 128], F32R) for k in range(2)]
        oht = pb("oht", [128, RING, 2, 128], BF16)
        ohs = pb("ohs", [128, RING, 2, 256], BF16)
        cm = pb("cm", [NB, 2])
        cr = pb("cr", [NB, 2])
        phase.close()

        agg2 = pb("agg2", [NB, NS, D + 1])
        src2 = pb("src2", [128, EC], I32)
        dst2 = pb("dst2", [128, EC], I32)
        srcf = pb("srcf", [128, EC])
        nodes = pb("nodes", [128, PASS, NB])
        ixb = pb("ixb", [128, 2, UN // 2], U32)
        grow = pb("grow", [128, UN, D + 1])
        oneh = pb("oneh", [128, 2, PASS * NB])
        rc = pb("rc", [NB, NS])
        rc0 = pb("rc0", [NB, NS])
        phase.close()

        w1_sb = pb("w1_sb", [128, 2, NE, H])
        w2_sb = pb("w2_sb", [H + 1, NE, D + 1])
        b1_sb = pb("b1_sb", [H, NE])
        hot_e = pb("hot_e", [NB, NS, NE])
        best = pb("best", [NB, NS])
        falling = pb("falling", [NB, NE])
        oe = pb("oe", [NB, NE, NS])
        oe2 = pb("oe2", [NB, NE, NS])
        place = hot_e.rearrange("p s e -> p (s e)").rearrange("p (e s) -> p e s", e=NE)
        fresh = pb("fresh", [NB, NE, NS])
        mine = pb("mine", [NB, NE], BF16)
        ones_b = pb("ones_b", [128, 128], BF16)
        earlier = pb("earlier", [128, 128], BF16)
        rb_sb = pb("rb_sb", [128, NE])
        tiles_f, tiles_to, tiles_from = (pb(n, [128, NE]) for n in ("tiles_f", "tiles_to", "tiles_from"))
        tiles_i = pb("tiles_i", [128, NE], I32)
        one_e = pb("one_e", [128, NE])
        shift = pb("shift", [NB, NE])
        below = pb("below", [128, NE])
        expert_f = pb("expert_f", [128, 1])
        tile_expert = pb("tile_expert", [1, 128], I32)
        slot_f = pb("slot_f", [NB, NS])
        slot_u = pb("slot_u", [NB, NS], U32)
        slot_ix = pb("slot_ix", [NB, 2, RG // 2], U32)
        rows = pb("rows", [NB, RG, D])
        xs = pb("xs", [128, 4, 2, D])
        xsT = pb("xsT", [128, 2, 2, 2, 128])
        w1_x = pb("w1_x", [128, 8, 2, H])
        w2_x = pb("w2_x", [H + 1, 8, D + 1])
        hT = pb("hT", [H + 1, 2, 2, 128])
        ys = pb("ys", [128, 4, 2, D])
        phase.close()

        s_in, s_w, s_id, s_c = sem("s_in"), sem("s_w"), sem("s_id"), sem("s_c")
        v_bias, v_st, v_ag, v_rs, v_xn = sem("v_bias"), sem("v_st"), sem("v_ag"), sem("v_rs"), sem("v_xn")
        p_b, pe_tr, a_xt2, pe_kv, pe_yz = sem("p_b"), sem("pe_tr"), sem("a_xt2"), sem("pe_kv"), sem("pe_yz")
        a_kx, v_kf, a_v, a_y, v_base, pe_cx = (sem(n) for n in (
            "a_kx", "v_kf", "a_v", "a_y", "v_base", "pe_cx"))
        v_cx, v_bd, pe_ct, v_ct, pe_m, v_m = (sem(n) for n in (
            "v_cx", "v_bd", "pe_ct", "v_ct", "pe_m", "v_m"))
        pe_q, a_ql, a_qp, a_at, a_qx, v_qf, pe_dn, v_dn, v_rc, v_qs, pe_at, v_at = (sem(n) for n in (
            "pe_q", "a_ql", "a_qp", "a_at", "a_qx", "v_qf", "pe_dn", "v_dn", "v_rc", "v_qs", "pe_at", "v_at"))
        s_e, p_ix, v_sub, v_oh, pe_e, v_agg = (sem(n) for n in (
            "s_e", "p_ix", "v_sub", "v_oh", "pe_e", "v_agg"))
        g_in = [sem(f"g_in{k}") for k in range(UN)]
        p_ve, p_k = sem("p_ve"), sem("p_k")
        s_rt, s_ew, f_st, f_ag, f_rs, f_xf, f_tr, f_xt, f_lg, f_lb, v_wx = (sem(n) for n in (
            "s_rt", "s_ew", "f_st", "f_ag", "f_rs", "f_xf", "f_tr", "f_xt", "f_lg", "f_lb", "v_wx"))
        z_out, f_mean, f_oe, f_oe2, f_cnt, pe_cnt, f_ecol, pe_ecol, f_te, f_slot = (sem(n) for n in (
            "z_out", "f_mean", "f_oe", "f_oe2", "f_cnt", "pe_cnt", "f_ecol", "pe_ecol", "f_te", "f_slot"))
        p_sx, f_row, pe_xs, a_xs, p_wx, pe_hid, v_hid, pe_ys, a_ys, f_y, f_out = (sem(n) for n in (
            "p_sx", "f_row", "pe_xs", "a_xs", "p_wx", "pe_hid", "v_hid", "pe_ys", "a_ys", "f_y", "f_out"))
        sc_out = [sem(f"sc_out{k}") for k in range(RG)]
        re_in = [sem(f"re_in{k}") for k in range(RG)]
        xs_in = [sem(f"xs_in{k}") for k in range(4)]
        ys_out = [sem(f"ys_out{k}") for k in range(4)]
        alone_v, alone_gp = sem("alone_v"), sem("alone_gp")

        r_ld, r_pad, r_v, pe_base, r_fit, pe_fit = (sem(n) for n in (
            "r_ld", "r_pad", "r_v", "pe_base", "r_fit", "pe_fit"))
        r_oh, r_pre, pe_rk, r_prod, r_r, r_ohr, p_val, pe_rt, a_rv, r_ready = (sem(n) for n in (
            "r_oh", "r_pre", "pe_rk", "r_prod", "r_r", "r_ohr", "p_val", "pe_rt", "a_rv", "r_ready"))
        w_ix, a_hi, v_lo, v_o, pe_a, a_cn, pe_d, v_cm, v_cr, v_ev, x1_ready = (sem(n) for n in (
            "w_ix", "a_hi", "v_lo", "v_o", "pe_a", "a_cn", "pe_d", "v_cm", "v_cr", "v_ev", "x1_ready"))
        p_one, b_rc, b_x1, q_c = sem("p_one"), sem("b_rc"), sem("b_x1"), sem("q_c")
        s_wr, a_wh, p_wl, v_xl, a_rl, a_xh, r_prep = (sem(n) for n in (
            "s_wr", "a_wh", "p_wl", "v_xl", "a_rl", "a_xh", "r_prep"))
        s_rb = sem("s_rb")
        y_out = [sem(f"y_out{k}") for k in range(2)]
        w_in = g_in

        x_v = x.rearrange("(b s) d -> b s d", s=NS)
        y_v = y_table.rearrange("(b s) d -> b s d", s=NS)
        o_v = out.rearrange("(b s) d -> b s d", s=NS)
        in_v = tokens_in.rearrange("(t p) d -> p t d", p=128)
        out_v = tokens_out.rearrange("(t p) d -> p t d", p=128)
        HALVES = ((0, 112), (112, NB))

        block = ctx.enter_context(nc.Block())

        def load_edges(eng, t_src, t_dst, done):
            last = E - (NG - 1) * GE
            rows = last // GC
            for t, w in ((t_src, src), (t_dst, dst)):
                eng.dma_start(t[:, 0:(NG - 1) * GC].rearrange("p (g c) -> p g c", c=GC),
                              w[0:(NG - 1) * GE].rearrange("(g p c) -> p g c", p=128, c=GC)).then_inc(done, 16)
                eng.dma_start(t[0:rows, (NG - 1) * GC:EC],
                              w[(NG - 1) * GE:(NG - 1) * GE + rows * GC].rearrange("(p c) -> p c", c=GC)).then_inc(done, 16)
                eng.dma_start(t[rows:rows + 1, (NG - 1) * GC:(NG - 1) * GC + last - rows * GC],
                              w[(NG - 1) * GE + rows * GC:E].rearrange("(p c) -> p c", p=1)).then_inc(done, 16)

        @block.sync
        def _(sp):
            sp.wait_ge(r_pad, 3)
            load_edges(sp, src_i, dst_i, r_ld)
            for k, w in enumerate((wkv, wyz)):
                sp.dma_start(w_raw[:, k], w.rearrange("(c p) o -> p c o", p=128)).then_inc(s_wr, 16)
            for t, w in ((wq_sb, wq), (wp_sb, wproj)):
                sp.dma_start(t[:], w.rearrange("(c p) o -> p c o", p=128)).then_inc(s_w, 16)
            sp.dma_start(bias_sb[:], bias3.rearrange("a d -> () a d").to_broadcast([128, 3, D])).then_inc(s_w, 16)
            for a, b in HALVES:
                sp.dma_start(x_sb[a:b], x_v[a:b]).then_inc(s_in, 16)
            for k in range(2):
                sp.dma_start(tokens_in.rearrange("(p t) d -> p (t d)", t=TT)[:, k * CH * D:(k + 1) * CH * D].rearrange("p (a d) -> p a d", d=D),
                             zeros[:].rearrange("p (a d) -> p a d", a=1).to_broadcast([128, CH, D])).then_inc(z_out, 16)

            def store_y(s, par):
                sp.wait_ge(a_y, s + 1)
                sp.dma_start(y_v[:, bass.ds(s, 1), :], yz[:, par:par + 1, 0:D]).then_inc(y_out[par], 16)

            run(sp, NS, [(0, store_y)])
            sp.wait_ge(z_out, 32)
            for k in range(2):
                sp.wait_ge(y_out[k], 16 * NS // 2)
            sp.wait_ge(v_at, G)
            sp.dma_start(rw_sb[:], rw.rearrange("(c p) o -> p c o", p=128)).then_inc(s_rt, 16)
            sp.wait_ge(x1_ready, 1)
            sp.dma_start(rb_sb[:], rb.rearrange("n -> () n").to_broadcast([128, NE])).then_inc(s_rb, 16)
            for c in range(2):
                sp.dma_start(w1_sb[:, c], w1[:, c * 128:(c + 1) * 128].rearrange("e p h -> p e h")).then_inc(s_ew, 16)
            sp.dma_start(w2_sb[0:H, :, 0:D], w2.rearrange("e h d -> h e d")).then_inc(s_ew, 16)
            sp.dma_start(w2_sb[H:H + 1, :, 0:D], b2.rearrange("e d -> () e d")).then_inc(s_ew, 16)
            sp.dma_start(b1_sb[:], b1).then_inc(s_ew, 16)

            def load(c, k, r):
                wait(sp, pe_xs, c - 3)
                sp.dma_start(xs[:, k], in_v[:, bass.ds(c * 2, 2)]).then_inc(xs_in[k], 16)

            for k in range(RG):
                sp.wait_ge(sc_out[k], 16 * NS // RG)
            run4(sp, CH, [(0, load)])
            for k in range(5):
                sp.wait_ge(f_y, 10 * (k + 1))
                for a, b in HALVES:
                    sp.dma_start(o_v[a:b, 10 * k:10 * k + 10], x_sb[a:b, 10 * k:10 * k + 10]).then_inc(f_out, 16)
            sp.wait_ge(f_out, 160)

        @block.gpsimd
        def _(gp):
            gp.memset(src_i[:], -1).then_inc(r_pad, 1)
            gp.memset(dst_i[:], 0).then_inc(r_pad, 1)
            gp.memset(zeros[:], 0.0).then_inc(r_pad, 1)
            gp.memset(ident[:], 0.0).then_inc(q_c, 1)
            gp.memset(ident_b[:], 0.0).then_inc(q_c, 1)
            gp.memset(before[:], 1.0).then_inc(q_c, 1)
            gp.memset(ones_f[:], 1.0).then_inc(q_c, 1)
            gp.memset(restart[:], 1.0).then_inc(q_c, 1)
            gp.memset(mhalf[:], -0.5).then_inc(q_c, 1)
            gp.wait_ge(q_c, 6)
            for m in (ident, ident_b):
                gp.affine_select(out=m[:], in_=m[:], compare_op=ALU.not_equal, fill=1.0, base=0,
                                 pattern=[[-1, 128]], channel_multiplier=1).then_inc(q_c, 1)
            gp.affine_select(out=before[:], in_=before[:], compare_op=ALU.is_gt, fill=0.0, base=0,
                             pattern=[[1, 128]], channel_multiplier=-1).then_inc(q_c, 1)
            gp.memset(restart[:].rearrange("p (i c) -> p i c", c=GC)[:, :, 0:1], 0.0).then_inc(q_c, 1)
            for t, pattern, base, mult in ((iota_b, [[1, 256]], 1, 0), (iota_r, [[1, 128], [0, GC]], 0, 0),
                                           (iota_i, [[1, NI], [0, GC]], 0, 0), (pcol, [[1, 1]], 0, 1)):
                gp.iota(t[:], pattern, base=base, channel_multiplier=mult, allow_small_or_imprecise_dtypes=True).then_inc(q_c, 1)

            gp.memset(hm0[:], 1.0).then_inc(s_id, 1)
            gp.memset(vv[:], 1.0).then_inc(s_id, 1)
            gp.wait_ge(s_id, 2)
            gp.affine_select(out=hm0[:].rearrange("p (a b) -> p a b", b=DH), in_=hm0[:].rearrange("p (a b) -> p a b", b=DH),
                             compare_op=ALU.is_ge, fill=0.0, base=0,
                             pattern=[[-DH, 128 // DH], [0, DH]], channel_multiplier=1).then_inc(s_id, 1)
            gp.wait_ge(s_id, 3)
            gp.affine_select(out=hmask[:].rearrange("p (a b) -> p a b", b=DH), in_=hm0[:].rearrange("p (a b) -> p a b", b=DH),
                             compare_op=ALU.is_ge, fill=0.0, base=DH - 1,
                             pattern=[[DH, 128 // DH], [0, DH]], channel_multiplier=-1).then_inc(s_id, 1)

            def root1(s, par):
                gp.wait_ge(v_ag, s + 1)
                gp.sem_inc(alone_gp, 1)
                gp.tensor_scalar(ve[:, par:par + 1], mv[:, par, 1:2], EPS, None, ALU.add).then_inc(p_ve, 1)
                gp.wait_ge(p_ve, s + 1)
                wait(gp, v_xn, s - 1)
                gp.tensor_tensor(rs[:, par:par + 1], ve[:, par:par + 1], mhalf[0:NB], ALU.pow).then_inc(v_rs, 1)

            def add_bias(s, par):
                gp.wait_ge(v_xn, s + 1)
                gp.tensor_tensor(x_sb[:, s, :], x_sb[:, s, :], bias[0:NB], ALU.add).then_inc(p_b, 1)

            def add_root(s, par):
                gp.wait_ge(a_y, s + 1)
                gp.wait_ge(p_b, s + 1)
                gp.tensor_tensor(x_sb[:, s, :], x_sb[:, s, :], yz[:, par, D:2 * D], ALU.add).then_inc(v_base, 1)

            def values(g, par):
                gp.wait_ge(r_oh, g + 1)
                wait(gp, pe_rt, g - 1)
                for k, t in enumerate((vd, vs)):
                    col = t[:, bass.ds(g * GC, GC)].rearrange("p (a c) -> p a c", a=1).to_broadcast([128, NI, GC])
                    gp.tensor_tensor(vals[par][:, k], ohI[par].rearrange("p (i c) -> p i c", c=GC), col, ALU.mult).then_inc(p_val, 1)

            for k, (h, l) in enumerate(((wkv_h, wkv_l), (wyz_h, wyz_l))):
                gp.wait_ge(a_wh, k + 1)
                gp.tensor_tensor(l, w_raw[:, k], h.bitcast(F32), ALU.subtract).then_inc(p_wl, 1)
            gp.wait_ge(s_w, 48)
            gp.tensor_tensor(biast, bias_sb[:, 0], bias_sb[:, 1], ALU.add).then_inc(v_bias, 1)
            gp.wait_ge(v_bias, 1)
            gp.tensor_tensor(bias, biast, bias_sb[:, 2], ALU.add).then_inc(v_bias, 1)
            gp.wait_ge(v_bias, 2)
            run_mixed(gp, [(0, NG, values), (AHEAD, NS, root1), (AHEAD + 1, NS, add_bias), (AHEAD + 3, NS, add_root)], AHEAD + 6)
            for k in range(2):
                gp.wait_ge(y_out[k], 16 * NS // 2)
            gp.wait_ge(z_out, 32)
            gp.wait_ge(r_fit, 1)

            def q_add(g, par):
                gp.wait_ge(a_qx, g + 1)
                gp.wait_ge(a_qp, g + 1)
                gp.tensor_tensor(qf[par], qf[par], qx[par], ALU.add).then_inc(v_qf, 1)

            def add_attention(g, par):
                gp.wait_ge(a_at, g + 1)
                pair = x_sb[:, bass.ds(g * 2, 2), :]
                gp.tensor_tensor(pair, pair, at[par], ALU.add).then_inc(v_at, 1)

            def windows(r, place):
                j = r * (RAW // 4) + place
                wait(gp, w_in[place], r * 64)
                gp.tensor_copy(wix[:, place, :], window_ix[:, bass.ds(j * 4, 4)]).then_inc(w_ix, 1)
                gp.wait_ge(w_ix, j + 1)
                for k in range(4):
                    wait(gp, v_lo, j * 4 + (k + 1 - RAW))
                    gp.sem_inc(alone_gp, 1)
                    gp.indirect_dma_start(raw[:, place * 4 + k, :], None, y_table,
                                          bass.IndirectOffsetOnAxis(ap=wix[:, place, k:k + 1], axis=0)).then_inc(w_in[place], 16)

            gp.wait_ge(v_base, NS)
            with gp.If(gp.value_load(fits[0:1, 0:1], min_val=0, max_val=1) == 1):
                for place in range(RAW // 4):
                    windows(0, place)
            run(gp, G, [(0, q_add), (4, add_attention)], peel=6)
            gp.wait_ge(v_at, G)
            fast = gp.value_load(fits[0:1, 0:1], min_val=0, max_val=1)
            with gp.If(fast == 1):
                gp.memset(y_hi[:, :, D:D + 2].bitcast(F32), 1.0).then_inc(p_one, 1)

                with gp.Fori(1, NG // RAW) as r:
                    for place in range(RAW // 4):
                        windows(r, place)
                for place in range(NG % RAW // 4):
                    windows(NG // RAW, place)
            with gp.If(fast == 0):
                gp.memset(src2[:], -1).then_inc(s_c, 1)
                gp.memset(dst2[:], 0).then_inc(s_c, 1)
                gp.memset(grow[:], 1.0).then_inc(s_c, 1)
                gp.iota(nodes[:], [[1, PASS], [NS, NB]], base=0, channel_multiplier=0,
                        allow_small_or_imprecise_dtypes=True).then_inc(s_c, 1)
                gp.wait_ge(s_c, 4)
                load_edges(gp, src2, dst2, s_e)
                gp.wait_ge(s_e, 96)

                def gather(it, j, first):
                    for hf in range(2):
                        if not first:
                            for k in range(UN // 2):
                                gp.wait_ge(g_in[hf * UN // 2 + k], it * 16)
                        gp.tensor_copy(ixb[:, hf, :], dst2[:, bass.ds(j * UN + hf * (UN // 2), UN // 2)]).then_inc(p_ix, 1)
                        gp.wait_ge(p_ix, it * 2 + hf + 1)
                        for k in range(UN // 2):
                            kk = hf * (UN // 2) + k
                            if not first:
                                gp.wait_ge(pe_e, it * UN - (UN - kk - 1))
                            gp.sem_inc(alone_gp, 1)
                            gp.indirect_dma_start(grow[:, kk, 0:D], None, y_table,
                                                  bass.IndirectOffsetOnAxis(ap=ixb[:, hf, k:k + 1], axis=0)
                                                  ).then_inc(g_in[kk], 16)

                STEPS = EC // UN
                gather(0, 0, True)
                with gp.Fori(1, STEPS) as j:
                    gather(j, j, False)
                with gp.Fori(1, NS // PASS) as r:
                    with gp.Fori(0, STEPS) as j:
                        gather(r * STEPS + j, j, False)
            def root(g, par):
                for t in range(2):
                    gp.wait_ge(f_ag, g * 2 + t + 1)
                    gp.sem_inc(alone_gp, 1)
                    gp.tensor_scalar(fve[:, t:t + 1], fmv[:, t, 1:2], EPS, None, ALU.add).then_inc(p_ve, 1)
                    gp.wait_ge(p_ve, g * 2 + t + 1 + NS)
                    gp.tensor_tensor(frs[:, bass.ds(g * 2 + t, 1)], fve[:, t:t + 1], mhalf[0:NB], ALU.pow).then_inc(f_rs, 1)

            run(gp, G, [(0, root)])
            gp.wait_ge(x1_ready, 1)
            gp.memset(w2_sb[H:H + 1, :, D:D + 1], 1.0).then_inc(p_k, 1)
            gp.memset(hT[H:H + 1], 1.0).then_inc(p_k, 1)
            gp.wait_ge(p_k, 2)
            gp.memset(one_e[:], 1.0).then_inc(p_k, 1)
            gp.memset(ones_b[:], 1.0).then_inc(p_k, 1)
            gp.memset(fresh[:], 1.0).then_inc(p_k, 1)
            gp.iota(falling[:], [[-1, NE]], base=NE, channel_multiplier=0, allow_small_or_imprecise_dtypes=True).then_inc(p_k, 1)
            gp.wait_ge(p_k, 6)
            gp.memset(fresh[:, :, 0:1], 0.0).then_inc(p_k, 1)
            gp.affine_select(out=earlier[:], in_=ones_b[:], compare_op=ALU.is_gt, fill=0.0, base=0,
                             pattern=[[1, 128]], channel_multiplier=-1).then_inc(p_k, 1)
            gp.wait_ge(s_ew, 80)
            gp.tensor_copy(w2_sb[0:H, :, D:D + 1].rearrange("p e a -> p (e a)"), b1_sb[:]).then_inc(p_k, 1)

            def indices(j, half, done, turn):
                for k in range(RG // 2):
                    wait(gp, done[half * (RG // 2) + k], j * 16)
                gp.tensor_copy(slot_ix[:, half], slot_u[:, bass.ds(j * RG + half * (RG // 2), RG // 2)]).then_inc(p_sx, 1)
                gp.wait_ge(p_sx, turn + j * 2 + half + 1)

            def send(j):
                for half in range(2):
                    indices(j, half, sc_out, 0)
                    for u in range(half * (RG // 2), (half + 1) * (RG // 2)):
                        gp.wait_ge(f_row, j * RG + u + 1)
                        gp.sem_inc(alone_gp, 1)
                        gp.indirect_dma_start(tokens_in, bass.IndirectOffsetOnAxis(ap=slot_ix[:, half, u % (RG // 2):u % (RG // 2) + 1], axis=0),
                                              rows[:, u, :], None).then_inc(sc_out[u], 16)

            gp.wait_ge(z_out, 32)
            gp.wait_ge(f_slot, 1)
            send(0)
            with gp.Fori(1, NS // RG) as j:
                send(j)

            def pick(c, k, r):
                for t in range(2):
                    e = gp.value_load(tile_expert[0:1, bass.ds(c * 2 + t, 1)], min_val=0, max_val=NE - 1)
                    wait(gp, pe_hid, c - 3)
                    gp.tensor_copy(w1_x[:, k * 2 + t], w1_sb[:, :, bass.ds(e, 1), :].rearrange("p c e h -> p c (e h)")).then_inc(p_wx, 1)

            gp.wait_ge(p_k, 9)
            gp.wait_ge(f_te, 1)
            run4(gp, CH, [(0, pick)])

            def fetch(j):
                for half in range(2):
                    indices(j, half, re_in, NS // RG * 2)
                    for u in range(half * (RG // 2), (half + 1) * (RG // 2)):
                        wait(gp, f_y, j * RG + (u + 1 - RG))
                        gp.sem_inc(alone_gp, 1)
                        gp.indirect_dma_start(rows[:, u, :], None, tokens_out,
                                              bass.IndirectOffsetOnAxis(ap=slot_ix[:, half, u % (RG // 2):u % (RG // 2) + 1], axis=0)
                                              ).then_inc(re_in[u], 16)

            for k in range(RG):
                gp.wait_ge(sc_out[k], 16 * NS // RG)
            for k in range(4):
                gp.wait_ge(ys_out[k], 16 * ((CH + 3 - k) // 4))
            fetch(0)
            with gp.Fori(1, NS // RG) as j:
                fetch(j)

        @block.scalar
        def _(act):
            def store_slots(g, par):
                act.wait_ge(pe_rt, g + 1)
                act.copy(routed[:, :, :, bass.ds(g, 1)].rearrange("p k i a -> p k (i a)"),
                         ps[:, 7, 0:2 * NI].rearrange("p (k i) -> p k i", k=2)).then_inc(a_rv, 1)

            def xt_high(s, par):
                act.wait_ge(pe_tr, s + 1)
                wait(act, pe_yz, s - 1)
                half = ps[:, 0, 0:250].rearrange("p (c n) -> p c n", c=2)
                act.copy(xt_h[:, par], half).then_inc(a_xh, 1)
                if isinstance(s, int) and s == 0:
                    act.wait_ge(r_prep, 1)
                    act.wait_ge(p_wl, 2)
                act.copy(xnT[:, :, bass.ds(s * NB, NB)], half).then_inc(a_xt2, 1)

            def kv_act(s, par):
                act.wait_ge(pe_kv, s + 1)
                wait(act, pe_cx, s - 1)
                act.copy(vv[:, par].rearrange("p (c n) -> p c n", c=2)[:, :, 0:128],
                         ps[0:NB, 2 + par, 256:512].rearrange("p (c n) -> p c n", c=2)).then_inc(a_v, 1)
                wait(act, v_kf, s - 1)
                act.activation(kx[:, par], ps[0:NB, 2 + par, 0:256], ACT.Relu, scale=-1.0).then_inc(a_rl, 1)
                act.wait_ge(pe_yz, s + 1)
                wait(act, v_base, s - 1)
                if isinstance(s, int):
                    wait(act, y_out[par], s // 2 * 16)
                else:
                    act.wait_ge(y_out[par], (s - par) * 8)
                act.copy(yz[:, par], ps[0:NB, 4 + par, :]).then_inc(a_y, 1)
                act.wait_ge(a_rl, s + 1)
                act.activation(kx[:, par], kx[:, par], ACT.Exp, scale=-1.0).then_inc(a_kx, 1)

            act.wait_ge(s_wr, 32)
            for k, h in enumerate((wkv_h, wyz_h)):
                act.copy(h, w_raw[:, k]).then_inc(a_wh, 1)
            act.wait_ge(s_id, 4)
            run_mixed(act, [(2, NG, store_slots), (AHEAD + 1, NS, xt_high), (AHEAD + 2, NS, kv_act)], AHEAD + 6)

            def q_exp(g, par):
                act.wait_ge(pe_q, g + 1)
                wait(act, v_qf, g - 1)
                act.activation(qx[par], ps[:, 2 + par, 0:500], ACT.Relu, scale=-1.0).then_inc(a_ql, 1)
                wait(act, pe_dn, g - 1)
                wait(act, v_qs, g - 1)
                act.activation(qf[par], ps[:, 2 + par, 0:500], ACT.Relu).then_inc(a_qp, 1)
                act.wait_ge(a_ql, g + 1)
                act.activation(qx[par], qx[par], ACT.Exp, scale=-1.0).then_inc(a_qx, 1)

            def keep_attention(g, par):
                act.wait_ge(pe_at, g + 1)
                wait(act, v_at, g - 1)
                act.copy(at[par].rearrange("p t d -> p (t d)"), ps[0:NB, 6 + par, :]).then_inc(a_at, 1)

            for k in range(2):
                act.wait_ge(y_out[k], 16 * NS // 2)
            act.wait_ge(v_base, NS)
            run(act, G, [(0, q_exp), (3, keep_attention)], peel=6)

            def high(q):
                for t in range(2):
                    w = 2 * q + t
                    act.wait_ge(w_in[w % RAW // 4], 64 * (w // RAW + 1))
                    act.copy(y_hi[:, w, 0:D], raw[:, w % RAW, :]).then_inc(a_hi, 1)

            def counts(n, par):
                act.wait_ge(pe_a, n + 1)
                wait(act, pe_d, n - 1)
                act.copy(cnt_T[par][:].rearrange("p t h n -> p (t h n)"), ps[:, par, :]).then_inc(a_cn, 1)

            def tokens(g):
                act.wait_ge(f_tr, g + 1)
                wait(act, f_lg, g)
                act.copy(xfT.rearrange("p c n -> p (c n)"), ps[:, 4, 0:500]).then_inc(f_xt, 1)

            act.wait_ge(v_at, G)
            fast = act.value_load(fits[0:1, 0:1], min_val=0, max_val=1)
            with act.If(fast == 1):
                for q in range(QP):
                    high(q)
                    if q >= 2:
                        counts(q - 2, q % 2)
                for q in range(QP - 2, QP):
                    counts(q, q % 2)
                def counts_of(i, beside=None):
                    for u in range(4):
                        counts(i * QP + u, u % 2)
                        if u == 0 and beside:
                            beside()
                    with act.Fori(1, QP // 4) as m:
                        for u in range(4):
                            counts(i * QP + m * 4 + u, u % 2)

                with act.Fori(1, 3) as i:
                    counts_of(i)
                counts_of(3, lambda: tokens(0))
                with act.Fori(4, NI) as i:
                    counts_of(i, lambda: tokens(i - 3))
                for g in range(NI - 3, G):
                    tokens(g)
            with act.If(fast == 0):
                tokens(0)
                with act.Fori(1, G) as g:
                    tokens(g)

            act.wait_ge(f_oe, 1)
            act.copy(oe2[:], oe[:]).then_inc(f_oe2, 1)

            def turned(c, k, r):
                act.wait_ge(pe_xs, c + 1)
                wait(act, pe_hid, c - 1)
                act.copy(xsT[:, k % 2].rearrange("p t c n -> p (t c n)"), ps[:, k % 2, :]).then_inc(a_xs, 1)

            def experts_out(c, k, r):
                act.wait_ge(pe_ys, c + 1)
                wait(act, ys_out[k], r * 16)
                act.activation(ys[:, k].rearrange("p t d -> p (t d)"), ps[:, 4 + k % 2, :], ACT.Relu).then_inc(a_ys, 1)

            def store(c, k, r):
                act.wait_ge(a_ys, c + 1)
                act.dma_start(out_v[:, bass.ds(c * 2, 2)], ys[:, k]).then_inc(ys_out[k], 16)

            run4(act, CH, [(0, turned), (2, experts_out), (3, store)])

        @block.tensor
        def _(pe):
            pe.wait_ge(q_c, 14)
            pe.wait_ge(r_v, 1)
            pe.matmul(ps[:, 4, 0:NG], ones_f[0:1, :], df[0:1, :].rearrange("p (g c) -> p g c", c=GC)[:, :, 0:1].rearrange("p g a -> p (g a)"),
                      start=True, stop=True).then_inc(pe_base, 1)

            def ranks(g, par):
                pe.wait_ge(r_pre, g + 1)
                wait(pe, r_prod, g)
                total = pre[par][:].rearrange("p (i c) -> p i c", c=GC)[:, :, GC - 1:GC].to_broadcast([128, NI, GC])
                pe.matmul(ps[:, 1, 0:NW], before[:], total, start=True, stop=False)
                pe.matmul(ps[:, 1, 0:NW], ident_b[:], pre[par][:], start=False, stop=True).then_inc(pe_rk, 1)

            def route(g, par):
                pe.wait_ge(r_ohr, g + 1)
                pe.wait_ge(p_val, g * 2 + 2)
                wait(pe, a_rv, g)
                for c in range(GC):
                    mm = pe.matmul(ps[:, 7, 0:2 * NI], ohr[par][:, :, c], vals[par][:, :, :, c].rearrange("p k i -> p (k i)"),
                                   start=(c == 0), stop=(c == GC - 1))
                mm.then_inc(pe_rt, 1)

            def tr(s, par):
                pe.wait_ge(v_xn, s + 1)
                wait(pe, v_xl, s)
                wait(pe, a_xt2, s)
                for c in range(2):
                    mm = pe.transpose(ps[:, 0, c * NB:(c + 1) * NB], xn[:, par, c * 128:(c + 1) * 128], ident[0:NB, 0:NB])
                mm.then_inc(pe_tr, 1)

            def project(out, par, w_h, w_l):
                for n, (t, w) in enumerate(((xt_h, w_h), (xt_h, w_l), (xt_l, w_h))):
                    for c in range(2):
                        mm = pe.matmul(out, t[:, par, c, :], w[:, c, :], start=(n == 0 and c == 0), stop=(n == 2 and c == 1))
                return mm

            def kvyz(s, par):
                pe.wait_ge(a_xh, s + 1)
                pe.wait_ge(v_xl, s + 1)
                wait(pe, v_kf, s - 1)
                wait(pe, a_v, s - 1)
                project(ps[0:NB, 2 + par, :], par, wkv_h, wkv_l).then_inc(pe_kv, 1)
                wait(pe, a_y, s - 1)
                project(ps[0:NB, 4 + par, :], par, wyz_h, wyz_l).then_inc(pe_yz, 1)

            def context(s, par):
                pe.wait_ge(v_kf, s + 1)
                pe.wait_ge(a_v, s + 1)
                for c in range(2):
                    mm = pe.matmul(ps[:, 6, c * 129:(c + 1) * 129], kf[:, par, c * 128:(c + 1) * 128], vv[:, par, c * 129:(c + 1) * 129],
                                   start=(isinstance(s, int) and s == 0 and c == 0), stop=(isinstance(s, int) and s == NS - 1),
                                   skip_group_check=True)
                mm.then_inc(pe_cx, 1)

            pe.wait_ge(s_id, 4)
            pe.wait_ge(p_wl, 2)
            run_mixed(pe, [(2, NG, route), (AHEAD + 4, NS, context), (AHEAD + 1, NS, tr), (AHEAD + 2, NS, kvyz), (0, NG, ranks)], AHEAD + 6)
            pe.wait_ge(r_ready, 1)
            pe.wait_ge(a_y, NS)
            pe.matmul(ps[0:1, 5, 0:1], good[:, 3:4], ones_f[:, 0:1], start=True, stop=True).then_inc(pe_fit, 1)
            pe.wait_ge(s_w, 48)
            pe.wait_ge(v_bd, 4)
            for c in range(2):
                mm = pe.transpose(ps[:, 0, c * 128:(c + 1) * 128], cbd[:, c, :], ident[:])
            mm.then_inc(pe_ct, 1)
            pe.wait_ge(v_ct, 1)
            for c in range(2):
                mm = pe.matmul(ps[:, 1, c * 256:(c + 1) * 256], cbdT[:, c, :], wp_sb[:, c, :], start=True, stop=True)
            mm.then_inc(pe_m, 1)

            def q(g, par):
                wait(pe, a_qp, g - 1)
                if isinstance(g, int) and g < 2:
                    pe.wait_ge(v_m, 1)
                    pe.wait_ge(a_xt2, NS)
                for o in range(2):
                    for c in range(2):
                        mm = pe.matmul(ps[:, 2 + par, o * 250:(o + 1) * 250], wq_sb[:, c, o * 128:(o + 1) * 128],
                                       xnT[:, c, bass.ds(g * 250, 250)], start=(c == 0), stop=(c == 1))
                mm.then_inc(pe_q, 1)

            def den(g, par):
                pe.wait_ge(v_qf, g + 1)
                wait(pe, v_dn, g - 1)
                for o in range(2):
                    mm = pe.matmul(ps[:, 4 + par, o * 250:(o + 1) * 250], ksb[:, o, :], qf[par][:, o * 250:(o + 1) * 250],
                                   start=True, stop=True)
                mm.then_inc(pe_dn, 1)

            def att(g, par):
                pe.wait_ge(v_qs, g + 1)
                wait(pe, a_at, g - 1)
                for t in range(2):
                    for o in range(2):
                        mm = pe.matmul(ps[0:NB, 6 + par, t * 256:(t + 1) * 256],
                                       qs[par][:, o * 250 + t * NB:o * 250 + (t + 1) * NB], msb[:, o, :],
                                       start=(o == 0), stop=(o == 1))
                mm.then_inc(pe_at, 1)

            run(pe, G, [(0, q), (3, att), (1, den)], peel=6)
            pe.wait_ge(v_at, G)

            def count(n, buf, par):
                pe.wait_ge(v_o, n + 1)
                wait(pe, a_cn, n - 1)
                for t in range(2):
                    mm = pe.matmul(ps[:, par, t * 256:(t + 1) * 256], oht[:, buf, t, :], ohs[:, buf, t, :], start=True, stop=True)
                mm.then_inc(pe_a, 1)

            def add_up(n, q, par, first, last):
                pe.wait_ge(a_cn, n + 1)
                for t in range(2):
                    g = q * 2 + t
                    for h in range(2):
                        w = cnt_T[par][:, t, h, 0:NB + 1]
                        pe.matmul(ps[0:NB + 1, 2 + h, 0:D + 2], w, y_hi[:, g, :], start=(first and t == 0), stop=False)
                        mm = pe.matmul(ps[0:NB + 1, 2 + h, 0:D], w, y_lo[:, g, :], start=False, stop=(last and t == 1))
                mm.then_inc(pe_d, 1)

            def block_sums(i, n0, windows, beside=None):
                def ready(q):
                    if windows:
                        pe.wait_ge(v_lo, q * 2 + 2)
                        if q == 0:
                            pe.wait_ge(p_one, 1)
                for q in range(4):
                    count(n0 + q, q, q % 2)
                    if q == 0 and beside:
                        beside()
                    if q:
                        if q == 1 and not windows:
                            pe.wait_ge(v_ev, i)
                        ready(q - 1)
                        add_up(n0 + (q - 1), q - 1, (q - 1) % 2, q == 1, False)
                with pe.Fori(1, QP // 4) as m:
                    for u in range(4):
                        count(n0 + m * 4 + u, u, u % 2)
                        if windows:
                            pe.wait_ge(v_lo, m * 8 + u * 2)
                        add_up(n0 + m * 4 + (u - 1), m * 4 + (u - 1), (u - 1) % 2, False, False)
                ready(QP - 1)
                add_up(n0 + (QP - 1), QP - 1, (QP - 1) % 2, False, True)

            def turn(g):
                pe.wait_ge(f_xf, g * 2 + 2)
                wait(pe, f_xt, g)
                for c in range(2):
                    for t in range(2):
                        mm = pe.transpose(ps[:, 4, c * 250 + t * NB:c * 250 + (t + 1) * NB], fxf[:, t, c * 128:(c + 1) * 128],
                                          ident[0:NB, 0:NB])
                mm.then_inc(f_tr, 1)

            def logits(g):
                pe.wait_ge(f_xt, g + 1)
                wait(pe, f_lb, g)
                for t in range(2):
                    for c in range(2):
                        mm = pe.matmul(ps[0:NB, 5, t * NE:(t + 1) * NE], xfT[:, c, t * NB:(t + 1) * NB], rw_sb[:, c, :],
                                       start=(c == 0), stop=(c == 1))
                mm.then_inc(f_lg, 1)

            pe.wait_ge(s_rt, 16)
            fast = pe.value_load(fits[0:1, 0:1], min_val=0, max_val=1)
            with pe.If(fast == 1):
                block_sums(0, 0, True)
                with pe.Fori(1, 3) as i:
                    block_sums(i, i * QP, False)
                block_sums(3, 3 * QP, False, lambda: turn(0))
                with pe.Fori(4, NI) as i:
                    def router():
                        logits(i - 4)
                        turn(i - 3)
                    block_sums(i, i * QP, False, router)
                for g in range(NI - 3, G):
                    logits(g - 1)
                    turn(g)
                logits(G - 1)

            def edges(it, first, last):
                for k in range(UN):
                    pe.wait_ge(g_in[k], it * 16 + 16)
                    pe.wait_ge(v_oh, it * UN + k + 1)
                    for c in range(PASS):
                        mm = pe.matmul(ps[0:NB, c, 0:D + 1], oneh[:, k % 2, c * NB:(c + 1) * NB], grow[:, k, :],
                                       start=(first and k == 0), stop=(last and k == UN - 1), skip_group_check=True)
                    mm.then_inc(pe_e, 1)

            STEPS = EC // UN
            with pe.If(fast == 0):
                pe.wait_ge(s_c, 4)
                def one_pass(r):
                    wait(pe, v_agg, r)
                    edges(r * STEPS, True, False)
                    with pe.Fori(1, STEPS - 1) as j:
                        edges(r * STEPS + j, False, False)
                    edges(r * STEPS + (STEPS - 1), False, True)

                one_pass(0)
                with pe.Fori(1, NS // PASS) as r:
                    one_pass(r)
                turn(0)
                logits(0)
                with pe.Fori(1, G) as g:
                    turn(g)
                    logits(g)

            pe.wait_ge(x1_ready, 1)
            pe.wait_ge(p_k, 8)
            pe.wait_ge(f_cnt, 1)
            pe.matmul(ps[0:NB, 4, 0:NE], earlier[0:NB, 0:NB], mine[:], start=True, stop=True)
            pe.matmul(ps[:, 4, NE:2 * NE], ones_b[0:NB, :], mine[:], start=True, stop=True).then_inc(pe_cnt, 1)
            pe.wait_ge(f_ecol, 1)
            pe.matmul(ps[0:1, 5, 0:128], expert_f[:], ident[:], start=True, stop=True).then_inc(pe_ecol, 1)

            def turn_sorted(c, k, r):
                pe.wait_ge(xs_in[k], r * 16 + 16)
                wait(pe, a_xs, c - 1)
                for t in range(2):
                    for h in range(2):
                        mm = pe.transpose(ps[:, k % 2, (t * 2 + h) * 128:(t * 2 + h + 1) * 128], xs[:, k, t, h * 128:(h + 1) * 128], ident[:])
                mm.then_inc(pe_xs, 1)

            def hidden(c, k, r):
                pe.wait_ge(a_xs, c + 1)
                pe.wait_ge(p_wx, c * 2 + 2)
                wait(pe, v_hid, (c - 1) * 2)
                for t in range(2):
                    for h in range(2):
                        mm = pe.matmul(ps[0:H, 2 + k % 2, t * 128:(t + 1) * 128], w1_x[:, k * 2 + t, h, :], xsT[:, k % 2, t, h, :],
                                       start=(h == 0), stop=(h == 1))
                mm.then_inc(pe_hid, 1)

            def outputs(c, k, r):
                pe.wait_ge(v_hid, c * 2 + 2)
                wait(pe, a_ys, c - 1)
                for t in range(2):
                    mm = pe.matmul(ps[:, 4 + k % 2, t * D:(t + 1) * D], hT[:, k % 2, t, :], w2_x[:, k * 2 + t, 0:D], start=True, stop=True)
                mm.then_inc(pe_ys, 1)

            pe.wait_ge(p_k, 9)
            pe.wait_ge(f_te, 1)
            run4(pe, CH, [(0, turn_sorted), (1, hidden), (2, outputs)])

        @block.vector
        def _(v):
            steps = [0]

            def then(ins):
                steps[0] += 1
                ins.then_inc(r_v, 1)
                v.wait_ge(r_v, steps[0])

            v.wait_ge(r_ld, 96)
            then(v.tensor_copy(df[:], dst_i[:]))
            then(v.tensor_copy(sf[:], src_i[:]))
            then(v.tensor_scalar(tf[:], sf[:], -(NS - 1) / 2, 1.0 / NS, ALU.add, ALU.mult))
            then(v.tensor_copy(bi[:], tf[:]))
            then(v.tensor_copy(bf[:], bi[:]))
            then(v.scalar_tensor_tensor(tile_f[:], bf[:], -float(NS), sf[:], ALU.mult, ALU.add))
            then(v.tensor_scalar(tf[:], tile_f[:], 0.5, -0.25, ALU.mult, ALU.add))
            then(v.tensor_copy(bi[:], tf[:]))
            then(v.tensor_copy(blk[:], bi[:]))
            then(v.scalar_tensor_tensor(tf[:], blk[:], -2.0, tile_f[:], ALU.mult, ALU.add))
            then(v.scalar_tensor_tensor(tf[:], tf[:], 128.0, bf[:], ALU.mult, ALU.add))
            then(v.tensor_scalar(vs[:], tf[:], 1.0, None, ALU.add))
            then(v.tensor_scalar(valid[:], sf[:], 0.0, None, ALU.is_ge))
            then(v.tensor_scalar(tf[:], valid[:], -1000.0, 1000.0, ALU.mult, ALU.add))
            then(v.tensor_tensor(blk[:], blk[:], tf[:], ALU.add))
            v.wait_ge(pe_base, 1)
            then(v.tensor_copy(base_f[:], ps[:, 4, 0:NG]))
            then(v.tensor_tensor(tf[:].rearrange("p (g c) -> p g c", c=GC), df[:].rearrange("p (g c) -> p g c", c=GC),
                                 base_f[:].rearrange("p (g a) -> p g a", a=1).to_broadcast([128, NG, GC]), ALU.subtract))
            then(v.tensor_scalar(vd[:], tf[:], 1.0, None, ALU.add))
            then(v.tensor_tensor(tf[:], tf[:], valid[:], ALU.mult))
            then(v.tensor_reduce(top[:, 0:1], tf[:], mybir.AxisListType.X, ALU.max))
            then(v.tensor_reduce(top[:, 1:2], tf[:], mybir.AxisListType.X, ALU.min))
            then(v.tensor_scalar(win_f[:], base_f[:], pcol[:, 0:1], float(N - 1), ALU.add, ALU.min))
            then(v.tensor_copy(window_ix[:], win_f[:]))
            v.wait_ge(q_c, 14)

            def hot_block(g, par):
                wait(v, p_val, g * 2 - 2)
                wait(v, r_prod, g - 1)
                col = blk[:, bass.ds(g * GC, GC)].rearrange("p (a c) -> p a c", a=1).to_broadcast([128, NI, GC])
                v.tensor_tensor(ohI[par].rearrange("p (i c) -> p i c", c=GC), col, iota_i.rearrange("p (i c) -> p i c", c=GC),
                                ALU.is_equal).then_inc(r_oh, 1)

            def count_own(g, par):
                v.wait_ge(r_oh, g + 1)
                wait(v, pe_rk, g - 1)
                v.sem_inc(alone_v, 1)
                v.tensor_tensor_scan(pre[par], restart, ohI[par], 0.0, ALU.mult, ALU.add).then_inc(r_pre, 1)

            def pick_rank(g, par):
                v.wait_ge(pe_rk, g + 1)
                wait(v, r_r, g - 1)
                v.scalar_tensor_tensor(prod[par], ps[:, 1, 0:NW], -1.0, ohI[par], ALU.add, ALU.mult).then_inc(r_prod, 1)

            def sum_rank(g, par):
                v.wait_ge(r_prod, g + 1)
                with nc.allow_low_precision(reason="one term is not zero, and ranks up to 256 are exact"):
                    v.tensor_reduce(rank[:, bass.ds(g * GC, GC)], prod[par].rearrange("p (i c) -> p c i", c=GC),
                                    mybir.AxisListType.X, ALU.add).then_inc(r_r, 1)

            def hot_rank(g, par):
                v.wait_ge(r_r, g + 1)
                wait(v, pe_rt, g - 1)
                col = rank[:, bass.ds(g * GC, GC)].rearrange("p (a c) -> p a c", a=1).to_broadcast([128, 128, GC])
                v.tensor_tensor(ohr[par], col, iota_r.rearrange("p (r c) -> p r c", c=GC), ALU.is_equal).then_inc(r_ohr, 1)

            def stats1(s, par):
                wait(v, v_rs, s - 1)
                v.sem_inc(alone_v, 1)
                v.bn_stats(st[:, par], x_sb[:, s, :]).then_inc(v_st, 1)

            def stats2(s, par):
                v.wait_ge(v_st, s + 1)
                wait(v, v_xn, s - 1)
                v.sem_inc(alone_v, 1)
                v.bn_aggr(mv[:, par], st[:, par]).then_inc(v_ag, 1)

            def norm(s, par):
                v.wait_ge(v_rs, s + 1)
                wait(v, pe_tr, s - 1)
                v.tensor_scalar(xn[:, par], x_sb[:, s, :], mv[:, par, 0:1], rs[:, par:par + 1], ALU.subtract, ALU.mult).then_inc(v_xn, 1)

            def xt_low(s, par):
                v.wait_ge(a_xt2, s + 1)
                wait(v, pe_yz, s - 1)
                v.tensor_tensor(xt_l[:, par], ps[:, 0, 0:250].rearrange("p (c n) -> p c n", c=2), xt_h[:, par].bitcast(F32),
                                ALU.subtract).then_inc(v_xl, 1)

            def keys(s, par):
                v.wait_ge(a_kx, s + 1)
                wait(v, pe_cx, s - 1)
                v.scalar_tensor_tensor(kf[:, par], ps[0:NB, 2 + par, 0:256], 0.0, kx[:, par], ALU.max, ALU.add).then_inc(v_kf, 1)

            v.wait_ge(s_in, 32)
            v.sem_inc(r_prep, 1)
            run_mixed(v, [(AHEAD + 1, NS, norm), (1, NG, pick_rank), (0, NG, hot_block), (1, NG, sum_rank), (AHEAD, NS, stats1),
                          (0, NG, count_own), (AHEAD + 1, NS, xt_low), (AHEAD, NS, stats2), (1, NG, hot_rank),
                          (AHEAD + 3, NS, keys)], AHEAD + 6)
            v.wait_ge(r_r, NG)
            then(v.tensor_reduce(top[:, 2:3], rank[:], mybir.AxisListType.X, ALU.max))
            then(v.tensor_scalar(good[:, 0:1], top[:, 0:1], 127.0, None, ALU.is_le))
            then(v.tensor_scalar(good[:, 1:2], top[:, 1:2], 0.0, None, ALU.is_ge))
            then(v.tensor_scalar(good[:, 2:3], top[:, 2:3], 127.0, None, ALU.is_le))
            then(v.tensor_tensor(good[:, 0:1], good[:, 0:1], good[:, 1:2], ALU.mult))
            v.tensor_tensor(good[:, 3:4], good[:, 0:1], good[:, 2:3], ALU.mult).then_inc(r_ready, 1)
            v.wait_ge(pe_fit, 1)
            v.tensor_scalar(fits[:], ps[0:1, 5, 0:1], 128.0, None, ALU.is_equal).then_inc(r_fit, 1)
            v.wait_ge(r_fit, 1)
            v.wait_ge(a_rv, NG)
            v.wait_ge(pe_cx, NS)
            v.wait_ge(s_id, 4)
            for c in range(2):
                v.tensor_copy(cx[:, c], ps[:, 6, c * 129:(c + 1) * 129]).then_inc(v_cx, 1)
            v.wait_ge(v_cx, 2)
            for c in range(2):
                v.tensor_tensor(cbd[:, c], cx[:, c, 0:128], hmask[:], ALU.mult).then_inc(v_bd, 1)
                v.tensor_scalar(ksb[:, c], hmask[:], cx[:, c, 128:129], None, ALU.mult).then_inc(v_bd, 1)
            v.wait_ge(pe_ct, 1)
            v.tensor_copy(cbdT[:].rearrange("p c n -> p (c n)"), ps[:, 0, 0:256]).then_inc(v_ct, 1)
            v.wait_ge(pe_m, 1)
            v.tensor_copy(msb[:].rearrange("p c n -> p (c n)"), ps[:, 1, :]).then_inc(v_m, 1)

            def q_scale(g, par):
                v.wait_ge(pe_dn, g + 1)
                wait(v, pe_at, g - 1)
                v.tensor_scalar(dn[par], ps[:, 4 + par, 0:500], 1e-6, None, ALU.max).then_inc(v_dn, 1)
                v.wait_ge(v_dn, g + 1)
                v.reciprocal(qr[par], dn[par]).then_inc(v_rc, 1)
                v.wait_ge(v_rc, g + 1)
                v.tensor_tensor(qs[par], qf[par], qr[par], ALU.mult).then_inc(v_qs, 1)

            run(v, G, [(0, q_scale)])
            v.wait_ge(v_at, G)

            def low(q):
                for t in range(2):
                    v.wait_ge(a_hi, 2 * q + t + 1)
                    v.tensor_tensor(y_lo[:, 2 * q + t, :], raw[:, (2 * q + t) % RAW, :], y_hi[:, 2 * q + t, 0:D].bitcast(F32),
                                    ALU.subtract).then_inc(v_lo, 1)

            def hot_slots(n, q, buf, i):
                wait(v, pe_a, n - (RING - 1))
                for t in range(2):
                    c = i * NG + q * 2 + t
                    v.tensor_scalar(oht[:, buf, t, :], iota_b[:, 0:128], routed[:, 0].rearrange("p i g -> p (i g)")[:, bass.ds(c, 1)],
                                    None, ALU.is_equal)
                    last = v.tensor_scalar(ohs[:, buf, t, :], iota_b[:], routed[:, 1].rearrange("p i g -> p (i g)")[:, bass.ds(c, 1)],
                                           None, ALU.is_equal)
                last.then_inc(v_o, 1)

            def means(i):
                v.wait_ge(pe_d, i * QP + QP)
                v.tensor_scalar(cm[:], ps[0:NB, 2:4, D], 1.0, None, ALU.max).then_inc(v_cm, 1)
                v.wait_ge(v_cm, i + 1)
                v.reciprocal(cr[:], cm[:]).then_inc(v_cr, 1)
                v.wait_ge(v_cr, i + 1)
                for h in range(2):
                    last = v.scalar_tensor_tensor(x_sb[:, i * 2 + h, :], ps[0:NB, 2 + h, 0:D], cr[:, h:h + 1], x_sb[:, i * 2 + h, :],
                                                  ALU.mult, ALU.add)
                last.then_inc(v_ev, 1)

            def stats(g):
                v.sem_inc(alone_v, 1)
                for t in range(2):
                    s = g * 2 + t
                    v.bn_stats(fst[:, t], x_sb[:, s, :]).then_inc(f_st, 1)
                    v.wait_ge(f_st, s + 1)
                    wait(v, f_rs, g * 2)
                    v.sem_inc(alone_v, 1)
                    v.bn_aggr(fmv[:, t], fst[:, t]).then_inc(f_ag, 1)
                v.wait_ge(f_ag, g * 2 + 2)
                v.tensor_copy(mean[:, bass.ds(g * 2, 2)], fmv[:, :, 0]).then_inc(f_mean, 1)

            def norm2(g):
                v.wait_ge(f_mean, g + 1)
                v.wait_ge(f_rs, g * 2 + 2)
                wait(v, f_tr, g)
                for t in range(2):
                    s = g * 2 + t
                    v.tensor_scalar(fxf[:, t], x_sb[:, s, :], mean[:, bass.ds(s, 1)], frs[:, bass.ds(s, 1)], ALU.subtract, ALU.mult).then_inc(f_xf, 1)

            def keep_logits(g):
                v.wait_ge(f_lg, g + 1)
                v.tensor_copy(lg[:, bass.ds(g * 2, 2), :], ps[0:NB, 5, 0:2 * NE].rearrange("p (t e) -> p t e", e=NE)).then_inc(f_lb, 1)

            fast = v.value_load(fits[0:1, 0:1], min_val=0, max_val=1)
            with v.If(fast == 1):
                for q in range(QP):
                    hot_slots(q, q, q % RING, 0)
                    low(q)
                def block_step(i, normed, routed_too):
                    for q in range(RING):
                        hot_slots(i * QP + q, q, q, i)
                    means(i - 1)
                    if normed:
                        norm2(i - 2)
                    v.wait_ge(v_ev, i)
                    stats(i - 1)
                    if routed_too:
                        keep_logits(i - 4)
                    with v.Fori(1, QP // RING) as m:
                        for u in range(RING):
                            hot_slots(i * QP + m * RING + u, m * RING + u, u, i)

                block_step(1, False, False)
                with v.Fori(2, 4) as i:
                    block_step(i, True, False)
                with v.Fori(4, NI) as i:
                    block_step(i, True, True)
                means(NI - 1)
                norm2(NI - 2)
                v.wait_ge(v_ev, NI)
                stats(NI - 1)
                keep_logits(NI - 4)
                keep_logits(NI - 3)
                norm2(NI - 1)
                keep_logits(NI - 2)
                keep_logits(NI - 1)
                v.wait_ge(v_ev, NI)
            with v.If(fast == 0):
                v.wait_ge(s_c, 4)
                v.wait_ge(s_e, 96)
                v.tensor_copy(srcf[:], src2[:]).then_inc(v_sub, 1)
                STEPS = EC // UN

                def hot(it, j):
                    for k in range(UN):
                        v.wait_ge(pe_e, it * UN + k - 1)
                        v.tensor_scalar(oneh[:, k % 2], nodes[:].rearrange("p a b -> p (a b)"),
                                        srcf[:, bass.ds(j * UN + k, 1)], None, ALU.is_equal).then_inc(v_oh, 1)

                def one_pass(r):
                    v.wait_ge(v_sub, r + 1)
                    for k in range(UN):
                        wait(v, pe_e, r * STEPS * UN + (k - 1 if k >= 2 else 0))
                        v.tensor_scalar(oneh[:, k % 2], nodes[:].rearrange("p a b -> p (a b)"), srcf[:, k:k + 1], None, ALU.is_equal).then_inc(v_oh, 1)
                    with v.Fori(1, STEPS) as j:
                        hot(r * STEPS + j, j)
                    v.wait_ge(pe_e, r * STEPS * UN + STEPS * UN)
                    v.tensor_copy(agg2[:, bass.ds(r * PASS, PASS), :], ps[0:NB, 0:PASS, 0:D + 1]).then_inc(v_agg, 1)
                    v.wait_ge(v_oh, r * STEPS * UN + STEPS * UN)
                    v.tensor_scalar(srcf[:], srcf[:], -float(PASS), None, ALU.add).then_inc(v_sub, 1)

                one_pass(0)
                with v.Fori(1, NS // PASS) as r:
                    one_pass(r)

                v.wait_ge(v_agg, NS // PASS)
                v.tensor_scalar(rc0[:], agg2[:, :, D], 1.0, None, ALU.max).then_inc(b_rc, 1)
                v.wait_ge(b_rc, 1)
                v.reciprocal(rc[:], rc0[:]).then_inc(b_rc, 1)
                v.wait_ge(b_rc, 2)
                with v.Fori(0, NS) as t:
                    v.scalar_tensor_tensor(x_sb[:, t, :], agg2[:, t, 0:D], rc[:, bass.ds(t, 1)], x_sb[:, t, :], ALU.mult, ALU.add).then_inc(b_x1, 1)
                v.wait_ge(b_x1, NS)

                def router(g):
                    stats(g)
                    norm2(g)
                    keep_logits(g)

                router(0)
                with v.Fori(1, G) as g:
                    router(g)
            v.sem_inc(x1_ready, 1)
            v.wait_ge(p_k, 7)
            v.wait_ge(f_lb, G)
            over_e = [NB, NS, NE]
            falling_e = falling.rearrange("p (a e) -> p a e", a=1).to_broadcast(over_e)
            best_e = best.rearrange("p (s a) -> p s a", a=1).to_broadcast(over_e)
            v.wait_ge(s_rb, 16)
            then(v.tensor_tensor(lg, lg, rb_sb[0:NB].rearrange("p (a e) -> p a e", a=1).to_broadcast(over_e), ALU.add))
            then(v.tensor_reduce(best, lg, mybir.AxisListType.X, ALU.max))
            then(v.tensor_tensor(hot_e, lg, best_e, ALU.is_equal))
            then(v.tensor_tensor(hot_e, hot_e, falling_e, ALU.mult))
            then(v.tensor_reduce(best, hot_e, mybir.AxisListType.X, ALU.max))
            v.tensor_tensor(oe, best.rearrange("p (a s) -> p a s", a=1).to_broadcast([NB, NE, NS]),
                            falling.rearrange("p (e a) -> p e a", a=1).to_broadcast([NB, NE, NS]), ALU.is_equal).then_inc(f_oe, 1)
            v.wait_ge(f_oe, 1)
            then(v.tensor_reduce(slot_f[:, 0:NE], oe, mybir.AxisListType.X, ALU.add))
            v.tensor_copy(mine, slot_f[:, 0:NE]).then_inc(f_cnt, 1)
            v.wait_ge(pe_cnt, 1)
            then(v.tensor_scalar(tiles_f, ps[:, 4, NE:2 * NE], 1.0 / 128, 127.0 / 256, ALU.mult, ALU.add))
            then(v.tensor_copy(tiles_i, tiles_f))
            then(v.tensor_copy(tiles_f, tiles_i))
            then(v.tensor_tensor_scan(tiles_to, one_e, tiles_f, 0.0, ALU.mult, ALU.add))
            then(v.tensor_tensor(tiles_from, tiles_to, tiles_f, ALU.subtract))
            then(v.tensor_scalar(below, tiles_to, pcol[:, 0:1], None, ALU.is_le))
            then(v.tensor_reduce(expert_f, below, mybir.AxisListType.X, ALU.add))
            v.tensor_scalar(expert_f, expert_f, float(NE - 1), None, ALU.min).then_inc(f_ecol, 1)
            then(v.scalar_tensor_tensor(shift, tiles_from[0:NB], 128.0, ps[0:NB, 4, 0:NE], ALU.mult, ALU.add))
            v.wait_ge(f_oe2, 1)
            then(v.scalar_tensor_tensor(oe2[:, :, 0:1], shift.rearrange("p (e a) -> p e a", a=1), -1.0, oe2[:, :, 0:1], ALU.add, ALU.add))
            flat = "p e s -> p (e s)"
            then(v.tensor_tensor_scan(place.rearrange(flat), fresh.rearrange(flat), oe2.rearrange(flat), 0.0, ALU.mult, ALU.add))
            then(v.tensor_tensor(place, place, oe, ALU.mult))
            then(v.tensor_reduce(slot_f, place.rearrange("p e s -> p s e"), mybir.AxisListType.X, ALU.add))
            v.tensor_copy(slot_u, slot_f).then_inc(f_slot, 1)
            v.wait_ge(pe_ecol, 1)
            v.tensor_copy(tile_expert, ps[0:1, 5, 0:128]).then_inc(f_te, 1)

            def norm_row(j):
                for u in range(RG):
                    s = j * RG + u
                    wait(v, sc_out[u], j * 16)
                    v.tensor_scalar(rows[:, u], x_sb[:, s, :], mean[:, bass.ds(s, 1)], frs[:, bass.ds(s, 1)], ALU.subtract, ALU.mult).then_inc(f_row, 1)

            v.wait_ge(f_mean, G)
            norm_row(0)
            with v.Fori(1, NS // RG) as j:
                norm_row(j)

            def pick(c, k, r):
                for t in range(2):
                    e = v.value_load(tile_expert[0:1, bass.ds(c * 2 + t, 1)], min_val=0, max_val=NE - 1)
                    wait(v, pe_ys, c - 3)
                    v.tensor_copy(w2_x[:, k * 2 + t], w2_sb[:, bass.ds(e, 1), :].rearrange("p e d -> p (e d)")).then_inc(v_wx, 1)

            def hidden_out(c, k, r):
                v.wait_ge(pe_hid, c + 1)
                v.wait_ge(v_wx, c * 2 + 2)
                wait(v, pe_ys, c - 1)
                for t in range(2):
                    v.tensor_scalar(hT[0:H, k % 2, t, :], ps[0:H, 2 + k % 2, t * 128:(t + 1) * 128], w2_x[0:H, k * 2 + t, D:D + 1], 0.0,
                                    ALU.add, ALU.max).then_inc(v_hid, 1)

            v.wait_ge(p_k, 9)
            v.wait_ge(f_te, 1)
            run4(v, CH, [(0, pick), (2, hidden_out)])

            def add_rows(j):
                for u in range(RG):
                    v.wait_ge(re_in[u], j * 16 + 16)
                    v.tensor_tensor(x_sb[:, j * RG + u, :], x_sb[:, j * RG + u, :], rows[:, u], ALU.add).then_inc(f_y, 1)

            add_rows(0)
            with v.Fori(1, NS // RG) as j:
                add_rows(j)


_OUT = ((N, D), "float32")


def kernel(**inputs):
    import numpy as np
    import concourse.bacc as bacc
    from concourse.bass_utils import run_bass_kernel_spmd as launch

    a = {k: np.asarray(v) for k, v in inputs.items()}
    lay = {
        "x": a["x"], "src": a["src"], "dst": a["dst"],
        "wkv": a["L0_mix_Wkv"].T, "wyz": np.concatenate([a["L0_gnn_W2"].T, a["L0_gnn_W1"].T], 1),
        "wq": a["L0_mix_Wq"].T, "wproj": a["L0_mix_Wproj"].T,
        "bias3": np.stack([a["L0_gnn_b1"], a["L0_gnn_b2"], a["L0_mix_bproj"]]),
        "rw": a["L0_ffn_router_w"].T, "rb": a["L0_ffn_router_b"],
        "w1": a["L0_ffn_W1"], "b1": a["L0_ffn_b1"].T, "w2": a["L0_ffn_W2"], "b2": a["L0_ffn_b2"],
    }
    nc = bacc.Bacc("TRN2", target_bir_lowering=False, num_devices=1)
    arrays, args = {}, []
    for name, v in lay.items():
        v = np.ascontiguousarray(v)
        arrays[f"in_{name}"] = v
        args.append(nc.dram_tensor(f"in_{name}", v.shape, mybir.dt.from_np(v.dtype), kind="ExternalInput").ap())
    args.append(nc.dram_tensor("out_0", _OUT[0], F32, kind="ExternalOutput").ap())
    gps_layer(nc, *args)
    r = launch(nc, [arrays], core_ids=[0])
    return r.results[0]["out_0"]
```
